# Optimizing a Trainium2 kernel written in Bass

```python
import numpy as np
import jax
import jax.numpy as jnp

def _softmax(x, axis=-1):
    return jax.nn.softmax(x, axis=axis)
def _gelu(x):
    return jax.nn.gelu(x, approximate=True)
def _silu(x):
    return jax.nn.silu(x)
def _sigmoid(x):
    return jax.nn.sigmoid(x)
def _layernorm(x, axis=-1, eps=1e-5):
    m = jnp.mean(x, axis=axis, keepdims=True)
    v = jnp.var(x, axis=axis, keepdims=True)
    return (x - m) / jnp.sqrt(v + eps)
def _scatter_add(tgt, idx, src, axis=0):
    return tgt.at[idx].add(src)
def _segment_sum(src, seg, n):
    return jax.ops.segment_sum(src, seg, n)

kernel_name = 'mk_conv_preact_d2_conv_nchw768_15608b'

def setup_inputs(seed: int = 0):
    np.random.seed(seed)
    _w = jnp.asarray
    def _rec_inputs():
        import jax
        import jax.numpy as jnp
        _gk = jax.random.key(seed)
        x = -0.0001538 + 1 * jax.random.normal(jax.random.fold_in(_gk, 1), (8, 768, 32, 32), jnp.float32)
        return x
    x = _rec_inputs()
    def _L0_conv_setup():
        import jax, jax.numpy as jnp
        import numpy as np
        NUM_HEADS = 12
        key = jax.random.key(seed)
        k1, k2, k3 = jax.random.split(key, 3)
        B, C, H, W = (8, 768, 32, 32)
        x = jax.random.normal(k1, (B, C, H, W), dtype=jnp.float32)
        W_qkv = jax.random.normal(k2, (3 * C, C), dtype=jnp.float32) * C ** (-0.5)
        W_proj = jax.random.normal(k3, (C, C), dtype=jnp.float32) * C ** (-0.5)
        b_proj = jnp.zeros((C,), dtype=jnp.float32)
        return {'x': x, 'W_qkv': W_qkv, 'W_proj': W_proj, 'b_proj': b_proj}
    _L0_conv_all = _L0_conv_setup()
    _L0_conv_in = {k: v for k, v in _L0_conv_all.items() if k in ('W_qkv', 'W_proj', 'b_proj', )}
    del _L0_conv_all

    def _L1_conv_setup():
        import jax, jax.numpy as jnp
        from jax import lax
        import numpy as np
        H = W = 64
        SCALE = 64.0
        STRIDE = 16
        CHAN_PER_POS = 16
        KSIZE = 3
        SIGMA = 0.5
        BATCH = 16

        def _init_offset_grid():
            offs = []
            n = 3
            for ih in range(-n, n + 1):
                for iw in range(-n, n + 1):
                    if ih == 0 and iw == 0:
                        continue
                    offs.append([iw * STRIDE / SCALE, ih * STRIDE / SCALE])
            return np.array(offs, dtype=np.float32)

        def _displace(x, offset):
            B, C, h, w = x.shape
            F_off = offset.shape[0]
            bind = C // F_off
            off_px = offset * SCALE
            off_int = lax.stop_gradient(jnp.round(off_px))
            sub = off_px - off_int
            dx = jnp.repeat(off_int[:, 0].astype(jnp.int32), bind)
            dy = jnp.repeat(off_int[:, 1].astype(jnp.int32), bind)
            iy = jnp.arange(h)[None, :] - dy[:, None]
            ix = jnp.arange(w)[None, :] - dx[:, None]
            vy = (iy >= 0) & (iy < h)
            vx = (ix >= 0) & (ix < w)
            iyc = jnp.clip(iy, 0, h - 1)
            ixc = jnp.clip(ix, 0, w - 1)
            ch = jnp.arange(C)
            shifted = x[:, ch[:, None, None], iyc[:, :, None], ixc[:, None, :]]
            mask = (vy[:, :, None] & vx[:, None, :]).astype(x.dtype)
            shifted = shifted * mask[None]
            r = jnp.arange(KSIZE, dtype=x.dtype) - KSIZE // 2
            fx = r[None, :]
            fy = r[:, None]
            kx = fx[None] + sub[:, 0][:, None, None]
            ky = fy[None] + sub[:, 1][:, None, None]
            kern = jnp.exp(-(kx * kx + ky * ky) / (2.0 * SIGMA * SIGMA))
            kern = kern / kern.sum(axis=(1, 2), keepdims=True)
            kern_c = jnp.repeat(kern, bind, axis=0)
            out = lax.conv_general_dilated(shifted, kern_c[:, None, :, :], window_strides=(1, 1), padding='SAME', feature_group_count=C, dimension_numbers=('NCHW', 'OIHW', 'NCHW'))
            return out
        key = jax.random.key(seed)
        k1, k2 = jax.random.split(key)
        C = 48 * CHAN_PER_POS
        x = jax.random.normal(k1, (BATCH, C, H, W), dtype=jnp.float32)
        offset = jnp.asarray(_init_offset_grid()) + 0.01 * jax.random.normal(k2, (48, 2), dtype=jnp.float32)
        return {'x': x, 'offset': offset}
    _L1_conv_all = _L1_conv_setup()
    _L1_conv_in = {k: v for k, v in _L1_conv_all.items() if k in ('offset', )}
    del _L1_conv_all

    return {
        "x": x,
        "L0_conv_W_qkv": _L0_conv_in["W_qkv"],
        "L0_conv_W_proj": _L0_conv_in["W_proj"],
        "L0_conv_b_proj": _L0_conv_in["b_proj"],
        "L1_conv_offset": _L1_conv_in["offset"],
    }

def reference(x, L0_conv_W_qkv, L0_conv_W_proj, L0_conv_b_proj, L1_conv_offset):
    import jax
    import jax.numpy as jnp
    def _L0_conv_ref(x, W_qkv, W_proj, b_proj):
        import jax, jax.numpy as jnp
        import numpy as np
        NUM_HEADS = 12
        B, C, H, W = x.shape
        N = H * W
        nh = NUM_HEADS
        hd = C // nh
        scale = hd ** (-0.5)
        x_flat = jnp.swapaxes(x.reshape(B, C, N), 1, 2)
        qkv = x_flat @ W_qkv.T
        qkv = qkv.reshape(B, N, 3, nh, hd).transpose(2, 0, 3, 1, 4)
        q, k, v = (qkv[0], qkv[1], qkv[2])
        var_v = jnp.var(v, axis=-1, ddof=1, keepdims=True)
        var_k = jnp.var(k, axis=-1, ddof=1, keepdims=True)
        scores = var_v @ jnp.swapaxes(var_k, -2, -1) * scale
        attn = jax.nn.softmax(scores, axis=-1)
        out = attn @ v
        out = jnp.swapaxes(out, 1, 2).reshape(B, N, C)
        out = out @ W_proj.T + b_proj
        return jnp.swapaxes(out, 1, 2).reshape(B, C, H, W)

    def _L1_conv_ref(x, offset):
        import jax, jax.numpy as jnp
        from jax import lax
        import numpy as np
        H = W = 64
        SCALE = 64.0
        STRIDE = 16
        CHAN_PER_POS = 16
        KSIZE = 3
        SIGMA = 0.5
        BATCH = 16

        def _init_offset_grid():
            offs = []
            n = 3
            for ih in range(-n, n + 1):
                for iw in range(-n, n + 1):
                    if ih == 0 and iw == 0:
                        continue
                    offs.append([iw * STRIDE / SCALE, ih * STRIDE / SCALE])
            return np.array(offs, dtype=np.float32)

        def _displace(x, offset):
            B, C, h, w = x.shape
            F_off = offset.shape[0]
            bind = C // F_off
            off_px = offset * SCALE
            off_int = lax.stop_gradient(jnp.round(off_px))
            sub = off_px - off_int
            dx = jnp.repeat(off_int[:, 0].astype(jnp.int32), bind)
            dy = jnp.repeat(off_int[:, 1].astype(jnp.int32), bind)
            iy = jnp.arange(h)[None, :] - dy[:, None]
            ix = jnp.arange(w)[None, :] - dx[:, None]
            vy = (iy >= 0) & (iy < h)
            vx = (ix >= 0) & (ix < w)
            iyc = jnp.clip(iy, 0, h - 1)
            ixc = jnp.clip(ix, 0, w - 1)
            ch = jnp.arange(C)
            shifted = x[:, ch[:, None, None], iyc[:, :, None], ixc[:, None, :]]
            mask = (vy[:, :, None] & vx[:, None, :]).astype(x.dtype)
            shifted = shifted * mask[None]
            r = jnp.arange(KSIZE, dtype=x.dtype) - KSIZE // 2
            fx = r[None, :]
            fy = r[:, None]
            kx = fx[None] + sub[:, 0][:, None, None]
            ky = fy[None] + sub[:, 1][:, None, None]
            kern = jnp.exp(-(kx * kx + ky * ky) / (2.0 * SIGMA * SIGMA))
            kern = kern / kern.sum(axis=(1, 2), keepdims=True)
            kern_c = jnp.repeat(kern, bind, axis=0)
            out = lax.conv_general_dilated(shifted, kern_c[:, None, :, :], window_strides=(1, 1), padding='SAME', feature_group_count=C, dimension_numbers=('NCHW', 'OIHW', 'NCHW'))
            return out
        return _displace(x, offset)

    def _gn(v, G=32, eps=1e-5):
        B_, C_, H_, W_ = v.shape
        g = v.reshape(B_, G, C_ // G, H_, W_)
        m = jnp.mean(g, axis=(2, 3, 4), keepdims=True)
        s = jnp.var(g, axis=(2, 3, 4), keepdims=True)
        return ((g - m) / jnp.sqrt(s + eps)).reshape(v.shape)

    def _ln_c(v, eps=1e-6):
        m = jnp.mean(v, axis=1, keepdims=True)
        s = jnp.var(v, axis=1, keepdims=True)
        return (v - m) / jnp.sqrt(s + eps)

    def _ln_t(v, eps=1e-5):
        m = jnp.mean(v, axis=-1, keepdims=True)
        s = jnp.var(v, axis=-1, keepdims=True)
        return (v - m) / jnp.sqrt(s + eps)

    def _to_tokens(v):
        B_, C_, H_, W_ = v.shape
        return v.reshape(B_, C_, H_ * W_).transpose(0, 2, 1)
    def _from_tokens(t, like):
        B_, C_, H_, W_ = like.shape
        return t.transpose(0, 2, 1).reshape(B_, C_, H_, W_)

    x = x + _L0_conv_ref(_gn(x), L0_conv_W_qkv, L0_conv_W_proj, L0_conv_b_proj)
    x = x + _L1_conv_ref(_gn(x), L1_conv_offset)
    return x


_drawn_inputs = setup_inputs


def setup_inputs(seed=0):
    import zlib

    import numpy as np

    out = dict(_drawn_inputs(seed))
    spreads = {'L0_conv_b_proj': (0.0, 0.1)}
    factors = {}
    for name, (base, spread) in spreads.items():
        noise = np.random.default_rng([zlib.crc32(name.encode()), seed]).standard_normal(out[name].shape)
        drawn = base * np.exp(spread * noise) if base else spread * noise
        out[name] = jnp.asarray(drawn.astype(out[name].dtype))
    for name, factor in factors.items():
        out[name] = (out[name] * factor).astype(out[name].dtype)
    return out
```

```python
from contextlib import ExitStack

import concourse.bass as bass
from concourse import mybir

F32 = mybir.dt.float32
F16 = mybir.dt.float16
I32 = mybir.dt.int32
ALU = mybir.AluOpType
ACT = mybir.ActivationFunctionType
AX_X = mybir.AxisListType.X
ABSMAX = bass.bass_isa.ReduceOp.absmax

P = 128


def gn_attention_displace(nc, x, w_qkv, w_proj, b_proj, offset, out):
    B, C, H, W = x.shape
    N = H * W
    CT = C // P
    MT = N // P
    HALF = 512
    NH = 12
    HD = C // NH
    NP = NH // 2
    G = 32
    GC = C // G
    F = offset.shape[0]
    FC = C // F
    FPT = P // FC
    MARGIN = H * W + W
    ROW = N + 2 * MARGIN
    EPS = 1e-5
    KV = 2 * C
    CH = KV // HALF
    HPC = HALF // HD
    RING = 8
    H_UP = 64.0
    W_TOP = 16384.0
    V_DOWN = 2.0 ** -19
    RND = 12582912.0
    NT = NP * MT * 2
    PU = 2 * CT
    KU = CH * MT

    x_t = x.rearrange("b (t p) h w -> b p t (h w)", p=P)
    out_t = out.rearrange("b (t p) h w -> b p t (h w)", p=P)

    def scratch(name, shape, dt=F32):
        return nc.dram_tensor(name, shape, dt, kind="Internal").ap()

    a_rows = scratch("a_rows", [NH, N])
    r_rows = scratch("r_rows", [2, N])
    shift_rows = scratch("shift_rows", [C, ROW])
    cs_rows = {k: scratch(f"cs_rows_{k}", [C, 2]) for k in "xy"}
    gs_rows = {k: scratch(f"gs_rows_{k}", [C, 2]) for k in "xy"}

    ctx = ExitStack()
    with ctx:
        def sb(name, shape, dt=F32):
            return ctx.enter_context(nc.sbuf_tensor(name, shape, dt))

        def sem(name):
            return ctx.enter_context(nc.semaphore(name))

        wkv = [sb(f"wkv_{n}", [P, CT, KV], F16) for n in ("hi", "lo")]
        wp = [sb(f"wp_{n}", [P, CT, C], F16) for n in ("hi", "lo")]
        h_sp = sb("h_sp", [P, CT, 2, N], F16)
        ox = sb("ox", [P, 2 * CT * N])
        o_sp = ox[:, 0:CT * N].bitcast(F16).rearrange("p (t s n) -> p t s n", t=CT, s=2)
        x1 = ox[:, CT * N:2 * CT * N].rearrange("p (t n) -> p t n", t=CT)
        vx = sb("vx", [P, CT * N])
        v_sb = vx[:, :].rearrange("p (m c) -> p m c", m=MT)
        x_in = vx[:, :].rearrange("p (t n) -> p t n", t=CT)
        ring = sb("ring", [P, RING, N])
        a_sb = sb("a_sb", [P, 4, N])
        h32 = h_sp[:, :, :, :].rearrange("p t s n -> p (t s n)").bitcast(F32).rearrange("p (t n) -> p t n", t=CT)
        acc = [h32[:, 0, :], h32[:, 1, :]]
        acc_pool = h32[:, 2, :]
        d_sb = h32[:, 3, :]
        r_sb = h32[:, 4, :]
        gn_t = [ring[:, i, :] for i in (0, 1)]
        sh_t = [ring[:, i, :] for i in (2, 3, 4)]
        tap_t = [ring[:, i, :] for i in (5, 6)]
        wkv_nat = ox[:, 0:KV // P * C].rearrange("p (r c) -> p r c", c=C)
        ring_flat = ring[:, :, :].rearrange("p r n -> p (r n)")
        wp_nat = ring_flat[:, 0:CT * C].rearrange("p (r c) -> p r c", c=C)
        zeros = ring_flat[:, 6 * N:6 * N + MARGIN]

        ident = sb("ident", [P, P])
        ones = sb("ones", [P, P])
        bias = sb("bias", [P, CT])
        taps = sb("taps", [P, CT, 2, 3])
        mask = sb("mask", [P, CT, W])
        starts_i = sb("starts_i", [1, F], I32)
        scale = sb("scale", [P, 2])
        cut_at = [0]

        def small(parts, *shape):
            n = 1
            for k in shape:
                n *= k
            v = a_sb[:, :, :].rearrange("p i n -> p (i n)")[0:parts, cut_at[0]:cut_at[0] + n]
            cut_at[0] += n
            if len(shape) == 2:
                v = v.rearrange("p (a b) -> p a b", b=shape[1])
            return v

        offc = small(P, CT, 2)
        offi = small(P, CT, 2)
        tsum = small(P, CT, 2)
        cols = small(P, W)
        mask2 = small(P, CT, W)
        offr = small(1, F, 2)
        offr2 = small(1, F, 2)
        starts = small(1, F)
        wmax = small(P, 4)
        wmax_all = small(P, 4)
        inv = sb("inv", [P, 2])
        var_f = sb("var_f", [P, 1])
        var_f8 = sb("var_f8", [P, 1])
        proj_f = sb("proj_f", [P, 1])
        st = sb("st", [P, MT, HPC, 6])
        dm = sb("dm", [P, MT, HPC])
        sq = sb("sq", [P, MT, HPC])
        m2 = sb("m2", [P, 2 * NH, MT])
        av = sb("av", [P, NH, MT])
        at = sb("at", [NH * MT, P])
        kmx = sb("kmx", [P, NH])
        kmx1 = sb("kmx1", [NH, 1])
        kdiag = sb("kdiag", [NH, NH])
        coef = sb("coef", [P, NH, MT])
        dt_sb = sb("dt_sb", [P, 2 * N // P])
        bst = {k: sb(f"bst_{k}", [P, CT, 2, 6]) for k in "xy"}
        mv = {k: sb(f"mv_{k}", [P, CT, 2]) for k in "xy"}
        gin = {k: sb(f"gin_{k}", [G, GC, 2]) for k in "xy"}
        gd = {k: sb(f"gd_{k}", [G, GC]) for k in "xy"}
        gq = {k: sb(f"gq_{k}", [G, GC]) for k in "xy"}
        gs = {k: sb(f"gs_{k}", [G, 6]) for k in "xy"}
        gout = {k: sb(f"gout_{k}", [G, GC, 2]) for k in "xy"}
        rb = {k: sb(f"rb_{k}", [P, CT, 2]) for k in "xy"}
        mhalf = sb("mhalf", [G, 1])

        ps = ctx.enter_context(nc.psum_tensor("ps", [P, 8, HALF], F32))
        work_bank = (0, 1, 4, 5)
        o_bank = ((0, 1), (2, 3), (6, 7))
        d_bank = (4, 5)
        ps_at = ps[0:NH * MT, 6, 0:P]
        ps_kt = ps[:, 7, 0:P]
        ps_km = ps[:, 7, P:P + NH]
        KH = ((0, 4), (4, NH))

        s_wkv_in = sem("s_wkv_in")
        s_wp_in = sem("s_wp_in")
        s_small_in = sem("s_small_in")
        s_ident = sem("s_ident")
        s_const = sem("s_const")
        s_zeros = sem("s_zeros")
        s_pads = sem("s_pads")
        s_wmax = sem("s_wmax")
        s_wall = sem("s_wall")
        s_scale = sem("s_scale")
        s_wt = sem("s_wt")
        s_whi = sem("s_whi")
        s_wlo = sem("s_wlo")
        s_sub = sem("s_sub")
        s_tapexp = sem("s_tapexp")
        s_starts = sem("s_starts")
        s_set = sem("s_set")
        s_xin = [sem(f"s_xin{t}") for t in range(CT)]
        s_bst = {k: sem(f"s_bst_{k}") for k in "xy"}
        s_stat = {k: sem(f"s_stat_{k}") for k in "xy"}
        s_cs = {k: sem(f"s_cs_{k}") for k in "xy"}
        s_gin = {k: sem(f"s_gin_{k}") for k in "xy"}
        s_gvar = {k: sem(f"s_gvar_{k}") for k in "xy"}
        s_pow = {k: sem(f"s_pow_{k}") for k in "xy"}
        s_gout = {k: sem(f"s_gout_{k}") for k in "xy"}
        s_gs = {k: sem(f"s_gs_{k}") for k in "xy"}
        s_rb = {k: sem(f"s_rb_{k}") for k in "xy"}
        s_gch = {k: sem(f"s_gch_{k}") for k in "xy"}
        s_hf = sem("s_hf")
        s_hhi = sem("s_hhi")
        s_hlo = sem("s_hlo")
        s_kv = sem("s_kv")
        s_bn = sem("s_bn")
        s_vev = sem("s_vev")
        s_ach = sem("s_ach")
        s_av = sem("s_av")
        s_atp = sem("s_atp")
        s_at = sem("s_at")
        s_arow = sem("s_arow")
        s_a = [sem(f"s_a{i}") for i in range(4)]
        s_kmx = sem("s_kmx")
        s_kch = sem("s_kch")
        s_ktp = sem("s_ktp")
        s_kdiag = sem("s_kdiag")
        s_kmp = sem("s_kmp")
        s_coef = sem("s_coef")
        s_exp = sem("s_exp")
        s_pv = sem("s_pv")
        s_acc = sem("s_acc")
        s_accp = sem("s_accp")
        s_d = sem("s_d")
        s_dsb = sem("s_dsb")
        s_dt = sem("s_dt")
        s_rt = sem("s_rt")
        s_rrow = sem("s_rrow")
        s_r = sem("s_r")
        s_on = sem("s_on")
        s_ohi = sem("s_ohi")
        s_olo = sem("s_olo")
        s_x1in = sem("s_x1in")
        s_xb = sem("s_xb")
        s_pj = sem("s_pj")
        s_x1 = sem("s_x1")
        s_gn = sem("s_gn")
        s_gst = [sem(f"s_gst{i}") for i in range(2)]
        s_sh = [sem(f"s_sh{i}") for i in range(3)]
        s_msk = sem("s_msk")
        s_tap = sem("s_tap")
        s_pch = sem("s_pch")
        s_fin = sem("s_fin")
        s_out = sem("s_out")

        s_held_sp, s_held_pool, s_held_dve = sem("s_held_sp"), sem("s_held_pool"), sem("s_held_dve")

        block = ctx.enter_context(nc.Block())

        def hold(eng, s):
            eng.sem_inc(s, 1)

        def run(eng, first, body, last):
            first()
            with eng.Fori(0, B - 1) as b:
                body(b)
            last(B - 1)

        POOL_M = 5
        DVE_ADDS = [(s, m) for m in range(1, MT) for s in (0, 1) if not (s == 1 and m >= POOL_M)]
        NDA = len(DVE_ADDS)
        NPA = MT - POOL_M - 1

        def add_index(s, m):
            if s == 1 and m >= POOL_M:
                return True, max(m, POOL_M + 1) - POOL_M - 1
            return False, DVE_ADDS.index((s, max(m, 1)))

        WU = (KV // P + CT) * CT // 3

        def w_unit(u):
            if u < KV // P * CT // 3:
                r, k = divmod(u, CT)
                return wkv, scale[:, 0:1], wkv_nat, k, r
            r, k = divmod(u - KV // P * CT // 3, CT)
            return wp, scale[:, 1:2], wp_nat, k, r

        PCH = 4 * CT
        ACH = 5 * CH

        def group_stats_dma(sp, k, b):
            sp.wait_ge(s_stat[k], b + 1)
            sp.dma_start(cs_rows[k].rearrange("(t p) s -> p t s", p=P), mv[k][:, :, :]).then_inc(s_cs[k], 16)
            sp.wait_ge(s_cs[k], b * 16 + 16)
            sp.dma_start(gin[k][:, :, :], cs_rows[k].rearrange("(g c) s -> g c s", c=GC)).then_inc(s_gin[k], 16)
            sp.wait_ge(s_gout[k], b + 1)
            sp.dma_start(gs_rows[k].rearrange("(g c) s -> g c s", c=GC), gout[k][:, :, :]).then_inc(s_gs[k], 16)
            sp.wait_ge(s_gs[k], b * 16 + 16)
            sp.dma_start(rb[k][:, :, :], gs_rows[k].rearrange("(t p) s -> p t s", p=P)).then_inc(s_rb[k], 16)

        GCH = 6

        def group_stats_dve(dve, k, b, up):
            n = [0]

            def link(ins):
                n[0] += 1
                ins.then_inc(s_gch[k], 1)
                dve.wait_ge(s_gch[k], b * GCH + n[0])

            mean, var = gin[k][:, :, 0], gin[k][:, :, 1]
            g = gs[k]
            dve.wait_ge(s_gin[k], b * 16 + 16)
            link(nc.vector.tensor_reduce(g[:, 0:1], mean, AX_X, ALU.add))
            link(nc.vector.tensor_scalar(g[:, 1:2], g[:, 0:1], 1.0 / GC, None, ALU.mult))
            link(nc.vector.tensor_scalar(gd[k][:, :], mean, g[:, 1:2], None, ALU.subtract))
            link(nc.vector.tensor_tensor(gq[k][:, :], gd[k][:, :], gd[k][:, :], ALU.mult))
            link(nc.vector.tensor_tensor(gd[k][:, :], gq[k][:, :], var, ALU.add))
            link(nc.vector.tensor_reduce(g[:, 2:3], gd[k][:, :], AX_X, ALU.add))
            assert n[0] == GCH
            nc.vector.tensor_scalar(g[:, 3:4], g[:, 2:3], 1.0 / GC, EPS, ALU.mult, ALU.add).then_inc(s_gvar[k], 1)
            dve.wait_ge(s_pow[k], b + 1)
            nc.vector.tensor_scalar(gout[k][:, :, 0], gd[k][:, :], 0.0, g[:, 4:5], ALU.mult, ALU.add)
            nc.vector.tensor_scalar(g[:, 5:6], g[:, 1:2], g[:, 4:5], -1.0, ALU.mult, ALU.mult).then_inc(s_gvar[k], 1)
            dve.wait_ge(s_gvar[k], b * 3 + 2)
            nc.vector.tensor_scalar(gout[k][:, :, 1], gd[k][:, :], 0.0, g[:, 5:6], ALU.mult, ALU.add).then_inc(s_gvar[k], 1)
            dve.wait_ge(s_gvar[k], b * 3 + 3)
            nc.vector.tensor_scalar(gout[k][:, :, :], gout[k][:, :, :], up, None, ALU.mult).then_inc(s_gout[k], 1)

        def group_pow(pool, k, b):
            pool.wait_ge(s_gvar[k], b * 3 + 1)
            nc.gpsimd.tensor_tensor(gs[k][:, 4:5], gs[k][:, 3:4], mhalf[:, :], ALU.pow).then_inc(s_pow[k], 1)

        @block.sync
        def _(sp):
            starts_v = []

            def chain_b(b):
                for t in range(CT):
                    sp.dma_start(x1[:, t, :], x_t[b, :, t, :]).then_inc(s_x1in, 16)
                for p in range(NP):
                    for h in (2 * p + 4, 2 * p + 5):
                        if h < NH:
                            sp.wait_ge(s_exp, b * NT + 2 * MT * (p + 1))
                            sp.dma_start(a_sb[:, h % 4, :], a_rows[h:h + 1, :].broadcast_to((P, N))).then_inc(s_a[h % 4], 16)
                    sp.wait_ge(s_dsb, b * NP + p + 1)
                    for s in (0, 1):
                        sp.dma_start(dt_sb[s * P // 2:(s + 1) * P // 2, :], d_sb[s * HD:s * HD + 1, :]).then_inc(s_dt, 16)
                    sp.wait_ge(s_rt, b * NP + p + 1)
                    sp.dma_start(r_rows.rearrange("s (a n) -> (s a) n", n=2 * N // P), dt_sb[:, :]).then_inc(s_rrow, 16)
                    sp.wait_ge(s_rrow, b * NP * 16 + 16 * (p + 1))
                    if p:
                        sp.wait_ge(s_olo, b * NP + p)
                    for s in (0, 1):
                        sp.dma_start(r_sb[s * HD:(s + 1) * HD, :],
                                     r_rows[s:s + 1, :].broadcast_to((HD, N))).then_inc(s_r, 16)

            def shift_in(b, t):
                sp.wait_ge(s_gst[t % 2], b * 48 + 16 * (t // 2 + 1))
                hold(sp, s_held_sp)
                if t >= 3:
                    sp.wait_ge(s_pch, b * PCH + 4 * (t - 3) + 2)
                hold(sp, s_held_sp)
                for f in range(FPT):
                    sp.dma_start(sh_t[t % 3][f * FC:(f + 1) * FC, :],
                                 shift_rows[t * P + f * FC:t * P + (f + 1) * FC,
                                            bass.ds(start_of(t * FPT + f), N)]).then_inc(s_sh[t % 3], 16)

            def start_of(f):
                return sp.value_load(starts_i[0:1, f:f + 1], min_val=0, max_val=2 * MARGIN)

            def layer1(b):
                group_stats_dma(sp, "y", b)
                for t in range(CT + 3):
                    if t < CT:
                        sp.wait_ge(s_gn, b * CT + t + 1)
                        sp.dma_start(shift_rows[t * P:(t + 1) * P, MARGIN:MARGIN + N], gn_t[t % 2]).then_inc(s_gst[t % 2], 16)
                    if 1 <= t <= CT:
                        shift_in(b, t - 1)
                    if t >= 3:
                        sp.wait_ge(s_fin, b * CT + t - 1)
                        hold(sp, s_held_sp)
                        sp.dma_start(out_t[b, :, t - 3, :], x1[:, t - 3, :]).then_inc(s_out, 16)
                sp.wait_ge(s_out, b * CT * 16 + CT * 16)
                hold(sp, s_held_sp)

            def first():
                sp.dma_start(wkv_nat[:, 0:CT, :], w_qkv[2 * C:3 * C, :].rearrange("(r p) c -> p r c", p=P)).then_inc(s_wkv_in, 16)
                sp.dma_start(wkv_nat[:, CT:2 * CT, :], w_qkv[C:2 * C, :].rearrange("(r p) c -> p r c", p=P)).then_inc(s_wkv_in, 16)
                sp.dma_start(wp_nat, w_proj.rearrange("(r p) c -> p r c", p=P)).then_inc(s_wp_in, 16)
                sp.dma_start(bias[:, :], b_proj.rearrange("(t p) -> p t", p=P), allow_slow_non_contiguous=True).then_inc(s_small_in, 16)
                sp.dma_start(offr[0:1, :, :], offset.rearrange("(a f) s -> a f s", a=1)).then_inc(s_small_in, 16)
                for t in range(CT):
                    for f in range(FPT):
                        n = t * FPT + f
                        sp.dma_start(offc[f * FC:(f + 1) * FC, t, :],
                                     offset[n:n + 1, :].broadcast_to((FC, 2))).then_inc(s_small_in, 16)
                sp.wait_ge(s_zeros, 1)
                for t in range(CT):
                    for at_ in (0, MARGIN + N):
                        sp.dma_start(shift_rows[t * P:(t + 1) * P, at_:at_ + MARGIN], zeros).then_inc(s_pads, 16)
                group_stats_dma(sp, "x", 0)
                sp.wait_ge(s_starts, 1)
                sp.wait_ge(s_pads, 2 * CT * 16)

            def body(b):
                chain_b(b)
                group_stats_dma(sp, "x", b + 1)
                layer1(b)

            def last(b):
                chain_b(b)
                layer1(b)

            run(sp, first, body, last)

        @block.gpsimd
        def _(pool):
            def make_h(b):
                group_pow(pool, "x", b)
                pool.wait_ge(s_rb["x"], b * 16 + 16)
                hold(pool, s_held_pool)
                for t in range(CT):
                    nc.gpsimd.tensor_scalar(x_in[:, t, :], x_in[:, t, :], rb["x"][:, t, 0:1], rb["x"][:, t, 1:2],
                                            ALU.mult, ALU.add).then_inc(s_hf, 1)

            def phase_b(b):
                pool.wait_ge(s_x1in, b * CT * 16 + CT * 16)
                hold(pool, s_held_pool)
                for t in range(CT):
                    nc.gpsimd.tensor_scalar(x1[:, t, :], x1[:, t, :], 1.0, bias[:, t:t + 1],
                                            ALU.mult, ALU.add).then_inc(s_xb, 1)
                for p in range(NP):
                    for m in range(POOL_M + 1, MT):
                        i = p * 2 * MT + 2 * m + 1
                        pool.wait_ge(s_exp, b * NT + i + 1)
                        n = m - POOL_M
                        if n == 1:
                            if p:
                                pool.wait_ge(s_d, b * NP + p)
                            one = ring[:, (i - 2) % RING, :]
                        else:
                            pool.wait_ge(s_accp, (b * NP + p) * NPA + n - 1)
                            one = acc_pool
                        nc.gpsimd.tensor_tensor(acc_pool, one, ring[:, i % RING, :], ALU.add).then_inc(s_accp, 1)
                    if p > 1:
                        o_first(b, p - 2)

            def o_first(b, p):
                pool.wait_ge(s_on, b * NP + p + 1)
                hold(pool, s_held_pool)
                nc.gpsimd.tensor_copy(o_sp[:, p, 0, :], r_sb).then_inc(s_ohi, 1)

            def layer1(b):
                group_pow(pool, "y", b)
                pool.wait_ge(s_rb["y"], b * 16 + 16)
                hold(pool, s_held_pool)
                for t in range(CT):
                    if t >= 2:
                        pool.wait_ge(s_gst[t % 2], b * 48 + 16 * (t // 2))
                        hold(pool, s_held_pool)
                    nc.gpsimd.tensor_scalar(gn_t[t % 2], x1[:, t, :], rb["y"][:, t, 0:1], rb["y"][:, t, 1:2],
                                            ALU.mult, ALU.add).then_inc(s_gn, 1)

            def first():
                nc.gpsimd.memset(zeros, 0.0).then_inc(s_zeros, 1)
                nc.gpsimd.memset(mhalf[:, :], -0.5).then_inc(s_const, 1)
                nc.gpsimd.memset(ones[:, :], 1.0).then_inc(s_const, 1)
                nc.gpsimd.memset(ident[:, :], 0.0).then_inc(s_ident, 1)
                nc.gpsimd.iota(cols, pattern=[[1, W]], base=0, channel_multiplier=0,
                               allow_small_or_imprecise_dtypes=True).then_inc(s_const, 1)
                pool.wait_ge(s_ident, 1)
                nc.gpsimd.affine_select(out=ident[:, :], in_=ident[:, :], compare_op=ALU.not_equal, fill=1.0,
                                        base=0, pattern=[[-1, P]], channel_multiplier=1).then_inc(s_ident, 1)
                pool.wait_ge(s_wmax, 4)
                nc.gpsimd.partition_all_reduce(wmax_all, wmax, P, ABSMAX).then_inc(s_wall, 1)
                pool.wait_ge(s_const, 3)
                make_h(0)

            def body(b):
                phase_b(b)
                make_h(b + 1)
                layer1(b)

            def last(b):
                phase_b(b)
                layer1(b)

            run(pool, first, body, last)

        @block.scalar
        def _(act):
            def make_h(b, room_free):
                for t in range(CT):
                    act.wait_ge(s_hf, b * CT + t + 1)
                    if t == 0 and room_free is not None:
                        act.wait_ge(s_ohi, room_free)
                        act.wait_ge(s_olo, room_free)
                    nc.scalar.activation(h_sp[:, t, 0, :], x_in[:, t, :], ACT.Copy).then_inc(s_hhi, 1)

            def load_x(b):
                for t in range(CT):
                    act.dma_start(x_in[:, t, :], x_t[b, :, t, :]).then_inc(s_xin[t], 16)

            def phase_a(b, layer1_b):
                for u in range(KU):
                    c, m = divmod(u, MT)
                    lo, hi = c * HALF, min((c + 1) * HALF, C)
                    if lo < hi:
                        act.wait_ge(s_bn, b * KU + u + 1)
                        nc.scalar.activation(v_sb[:, m, lo:hi], ps[:, work_bank[u % 4], 0:hi - lo], ACT.Copy,
                                             scale=V_DOWN).then_inc(s_vev, 1)
                    if u == 18:
                        act.wait_ge(s_atp, b + 1)
                        nc.scalar.activation(at[:, :], ps_at, ACT.Copy).then_inc(s_at, 1)
                        act.wait_ge(s_at, b + 1)
                        act.dma_start(a_rows.rearrange("h (m n) -> (h m) n", n=P), at[:, :]).then_inc(s_arow, 16)
                        act.wait_ge(s_arow, b * 16 + 16)
                        for h in range(4):
                            act.dma_start(a_sb[:, h, :], a_rows[h:h + 1, :].broadcast_to((P, N))).then_inc(s_a[h], 16)
                    if layer1_b is not None and u >= 5 and (u - 5) % 3 == 0 and (u - 5) // 3 < CT:
                        middle_tap(layer1_b, (u - 5) // 3)

            def last_o(b):
                for p in (NP - 2, NP - 1):
                    act.wait_ge(s_on, b * NP + p + 1)
                    nc.scalar.activation(o_sp[:, p, 0, :], r_sb, ACT.Copy).then_inc(s_ohi, 1)

            def middle_tap(b, t):
                act.wait_ge(s_msk, b * CT + t + 1)
                if t >= 2:
                    act.wait_ge(s_fin, b * CT + t)
                nc.scalar.activation(tap_t[t % 2], sh_t[t % 3], ACT.Copy,
                                     scale=taps[:, t, 1, 1:2]).then_inc(s_tap, 1)

            def phase_b(b):
                act.wait_ge(s_fin, b * CT + 1)
                for p in range(NP):
                    for m in range(MT):
                        for s in (0, 1):
                            h = 2 * p + s
                            i = (p * MT + m) * 2 + s
                            if s == 0 and m == 0 and p in (0, 2):
                                act.wait_ge(s_coef, b * 2 + p // 2 + 1)
                            if m == 0:
                                act.wait_ge(s_a[h % 4], b * 48 + 16 * (h // 4 + 1))
                            if i >= RING:
                                j = i - RING
                                pj, mj = divmod(j // 2, MT)
                                act.wait_ge(s_pv, b * (NT // 2) + j // 2 + 1)
                                by_pool, n = add_index(s, mj)
                                if by_pool:
                                    act.wait_ge(s_accp, (b * NP + pj) * NPA + n + 1)
                                else:
                                    act.wait_ge(s_acc, (b * NP + pj) * NDA + n + 1)
                            nc.scalar.activation(ring[:, i % RING, :], a_sb[:, h % 4, :], ACT.Exp,
                                                 scale=coef[:, h, m:m + 1]).then_inc(s_exp, 1)

            def first():
                load_x(0)
                act.wait_ge(s_sub, 1)
                nc.scalar.activation(taps[:, :, :, :], taps[:, :, :, :], ACT.Exp, scale=-2.0).then_inc(s_tapexp, 1)
                act.wait_ge(s_scale, 1)
                for u in range(WU):
                    dst, sc, t, k, r = w_unit(u)
                    act.wait_ge(s_wt, u + 1)
                    nc.scalar.activation(dst[0][:, k, r * 3 * P:(r + 1) * 3 * P], ps[:, work_bank[u % 4], 0:3 * P],
                                         ACT.Copy, scale=sc).then_inc(s_whi, 1)
                make_h(0, None)
                phase_a(0, None)

            def body(b):
                phase_b(b)
                act.wait_ge(s_pv, b * (NT // 2) + NT // 2)
                load_x(b + 1)
                last_o(b)
                make_h(b + 1, b * NP + NP)
                phase_a(b + 1, b)

            def last(b):
                phase_b(b)
                last_o(b)
                for t in range(CT):
                    middle_tap(b, t)

            run(act, first, body, last)

        @block.vector
        def _(dve):
            def channel_stats(k, t, halves, src):
                for j in halves:
                    nc.vector.bn_stats(bst[k][:, t, j, :], src[:, t, j * HALF:(j + 1) * HALF]).then_inc(s_bst[k], 1)

            def channel_aggregate(k, b):
                dve.wait_ge(s_bst[k], b * PU + PU)
                hold(dve, s_held_dve)
                for t in range(CT):
                    ins = nc.vector.bn_aggr(mv[k][:, t, :], bst[k][:, t, :, :].rearrange("p j s -> p (j s)"))
                ins.then_inc(s_stat[k], 1)

            def x_stats(b, tiles):
                for t in tiles:
                    dve.wait_ge(s_xin[t], b * 16 + 16)
                    channel_stats("x", t, (0, 1), x_in)

            def h_second(b, t):
                dve.wait_ge(s_hhi, b * CT + t + 1)
                nc.vector.tensor_tensor(h_sp[:, t, 1, :], x_in[:, t, :], h_sp[:, t, 0, :], ALU.subtract).then_inc(s_hlo, 1)

            def phase_a(b, layer1_b):
                n = [0]

                def link(ins, hold=True):
                    n[0] += 1
                    ins.then_inc(s_ach, 1)
                    if hold:
                        dve.wait_ge(s_ach, b * ACH + n[0])

                for u in range(KU):
                    c, m = divmod(u, MT)
                    dve.wait_ge(s_kv, b * KU + u + 1)
                    for g in range(HPC):
                        ins = nc.vector.bn_stats(st[:, m, g, :], ps[:, work_bank[u % 4], g * HD:(g + 1) * HD])
                    ins.then_inc(s_bn, 1)
                    if m == MT - 1:
                        dve.wait_ge(s_bn, b * KU + u + 1)
                        dst = m2[:, c * HPC:(c + 1) * HPC, :].rearrange("p g m -> p m g")
                        link(nc.vector.tensor_tensor(dm[:, :, :], st[:, :, :, 1], st[:, :, :, 4], ALU.subtract))
                        link(nc.vector.tensor_tensor(sq[:, :, :], dm[:, :, :], dm[:, :, :], ALU.mult))
                        link(nc.vector.tensor_tensor(dm[:, :, :], st[:, :, :, 2], st[:, :, :, 5], ALU.add))
                        link(nc.vector.tensor_scalar(sq[:, :, :], sq[:, :, :], HD / 4.0, None, ALU.mult))
                        link(nc.vector.tensor_tensor(dst, sq[:, :, :], dm[:, :, :], ALU.add))
                    if u == 2 * MT - 1:
                        nc.vector.tensor_scalar(av[:, :, :], m2[:, 0:NH, :], var_f[:, 0:1], None, ALU.mult).then_inc(s_av, 1)
                        k_partition_max(0)
                    if u == 19:
                        k_max(b, 0)
                    if u == 21:
                        k_scales(b, 0)
                    if layer1_b is not None and 5 <= u < 5 + 3 * CT:
                        layer1_part(layer1_b, (u - 5) // 3, (u - 5) % 3)
                k_partition_max(1)
                assert n[0] == ACH

            def k_partition_max(part):
                h0, h1 = KH[part]
                nc.vector.tensor_reduce(kmx[:, h0:h1], m2[:, NH + h0:NH + h1, :], AX_X, ALU.max).then_inc(s_kmx, 1)

            def k_max(b, part):
                h0, h1 = KH[part]
                dve.wait_ge(s_ktp, b * 2 + part + 1)
                nc.vector.tensor_reduce(kmx1[0:h1 - h0, :], ps_kt[0:h1 - h0, :], AX_X, ALU.max).then_inc(s_kch, 1)
                dve.wait_ge(s_kch, b * 4 + 2 * part + 1)
                nc.vector.tensor_scalar(kdiag[0:h1 - h0, 0:h1 - h0], ident[0:h1 - h0, 0:h1 - h0], kmx1[0:h1 - h0, 0:1],
                                        None, ALU.mult).then_inc(s_kdiag, 1)

            def k_scales(b, part):
                h0, h1 = KH[part]
                dve.wait_ge(s_kmp, b * 2 + part + 1)
                nc.vector.tensor_tensor(coef[:, h0:h1, :], m2[:, NH + h0:NH + h1, :],
                                        ps_km[:, 0:h1 - h0].unsqueeze(2).broadcast_to((P, h1 - h0, MT)),
                                        ALU.subtract).then_inc(s_kch, 1)
                dve.wait_ge(s_kch, b * 4 + 2 * part + 2)
                nc.vector.tensor_scalar(coef[:, h0:h1, :], coef[:, h0:h1, :], var_f8[:, 0:1], 0.0,
                                        ALU.mult, ALU.min).then_inc(s_coef, 1)

            def layer1_part(b, t, part):
                sh = sh_t[t % 3].rearrange("p (y x) -> p y x", x=W)
                tp = tap_t[t % 2].rearrange("p (y x) -> p y x", x=W)
                xt = x1[:, t, :].rearrange("p (y x) -> p y x", x=W)
                ky, kx = taps[:, t, 1, :], taps[:, t, 0, :]
                base = b * PCH + 4 * t

                def link(n, out_, in_, k):
                    nc.vector.scalar_tensor_tensor(out_, in_, k, out_, ALU.mult, ALU.add).then_inc(s_pch, 1)
                    dve.wait_ge(s_pch, base + n)

                if part == 0:
                    dve.wait_ge(s_sh[t % 3], b * 256 + 128 * (t // 3 + 1))
                    nc.vector.tensor_tensor(sh, sh, mask[:, t:t + 1, :].broadcast_to((P, H, W)), ALU.mult).then_inc(s_msk, 1)
                elif part == 1:
                    dve.wait_ge(s_tap, b * CT + t + 1)
                    link(1, tp[:, 1:H, :], sh[:, 0:H - 1, :], ky[:, 0:1])
                    link(2, tp[:, 0:H - 1, :], sh[:, 1:H, :], ky[:, 2:3])
                else:
                    link(3, xt, tp, kx[:, 1:2])
                    link(4, xt[:, :, 1:W], tp[:, :, 0:W - 1], kx[:, 0:1])
                    nc.vector.scalar_tensor_tensor(xt[:, :, 0:W - 1], tp[:, :, 1:W], kx[:, 2:3], xt[:, :, 0:W - 1],
                                                   ALU.mult, ALU.add).then_inc(s_fin, 1)

            def d_copy(b, p):
                dve.wait_ge(s_d, b * NP + p + 1)
                if p:
                    dve.wait_ge(s_dt, b * NP * 32 + 32 * p)
                nc.vector.tensor_copy(d_sb.rearrange("p (a n) -> p a n", a=2), ps[:, 4:6, :]).then_inc(s_dsb, 1)

            def d_reciprocal(b, p):
                dve.wait_ge(s_dt, b * NP * 32 + 32 * (p + 1))
                nc.vector.reciprocal(dt_sb[:, :], dt_sb[:, :]).then_inc(s_rt, 1)

            def o_normalise(b, p):
                dve.wait_ge(s_r, b * NP * 32 + 32 * (p + 1))
                r2 = r_sb.rearrange("p (a n) -> p a n", a=2)
                k = o_bank[p % 3][0]
                nc.vector.tensor_tensor(r2, ps[:, k:k + 2, :], r2, ALU.mult).then_inc(s_on, 1)

            def o_second(b, p):
                dve.wait_ge(s_ohi, b * NP + p + 1)
                nc.vector.tensor_tensor(o_sp[:, p, 1, :], r_sb, o_sp[:, p, 0, :], ALU.subtract).then_inc(s_olo, 1)

            def phase_b(b):
                for p in range(NP):
                    done = (b * NP + p) * NDA
                    for n, (s, m) in enumerate(DVE_ADDS):
                        i = (p * MT + m) * 2 + s
                        dve.wait_ge(s_exp, b * NT + i + 1)
                        if m == 1:
                            if p and s == 0:
                                dve.wait_ge(s_d, b * NP + p)
                            one = ring[:, (i - 2) % RING, :]
                        else:
                            dve.wait_ge(s_acc, done + add_index(s, m - 1)[1] + 1)
                            one = acc[s]
                        nc.vector.tensor_tensor(acc[s], one, ring[:, i % RING, :], ALU.add).then_inc(s_acc, 1)
                        if p == 0 and (s, m) == (0, 3):
                            k_max(b, 1)
                        if p == 0 and (s, m) == (0, 6):
                            k_scales(b, 1)
                        if p and (s, m) == (0, 2):
                            d_copy(b, p - 1)
                        if p > 1 and (s, m) == (0, 4):
                            o_normalise(b, p - 2)
                        if p > 1 and (s, m) == (0, 6):
                            o_second(b, p - 2)
                        if p and (s, m) == (0, 7):
                            d_reciprocal(b, p - 1)

            def group_end(b, with_next):
                d_copy(b, NP - 1)
                o_normalise(b, NP - 2)
                o_second(b, NP - 2)
                d_reciprocal(b, NP - 1)
                if with_next:
                    x_stats(b + 1, range(0, 6))
                    channel_aggregate("x", b + 1)
                o_normalise(b, NP - 1)
                o_second(b, NP - 1)
                for u in range(PU):
                    t, j = divmod(u, 2)
                    if u == 2 and with_next:
                        group_stats_dve(dve, "x", b + 1, H_UP)
                    dve.wait_ge(s_pj, b * PU + u + 1)
                    if u == 0:
                        dve.wait_ge(s_xb, b * CT + CT)
                    cut = x1[:, t, j * HALF:(j + 1) * HALF]
                    nc.vector.scalar_tensor_tensor(cut, ps[:, work_bank[u % 4], :], proj_f[:, 0:1], cut,
                                                   ALU.mult, ALU.add).then_inc(s_x1, 1)
                    if with_next and 4 <= u < 4 + CT:
                        h_second(b + 1, u - 4)
                    dve.wait_ge(s_x1, b * PU + u + 1)
                    channel_stats("y", t, (j,), x1)
                channel_aggregate("y", b)

            def first():
                n = [0]

                def link(ins):
                    n[0] += 1
                    ins.then_inc(s_set, 1)
                    dve.wait_ge(s_set, n[0])

                dve.wait_ge(s_wkv_in, 32)
                nc.vector.tensor_reduce(wmax[:, 0:1], ox[:, 0:KV // P * C], AX_X, ALU.max).then_inc(s_wmax, 1)
                nc.vector.tensor_reduce(wmax[:, 1:2], ox[:, 0:KV // P * C], AX_X, ALU.min).then_inc(s_wmax, 1)
                dve.wait_ge(s_wp_in, 16)
                nc.vector.tensor_reduce(wmax[:, 2:3], ring_flat[:, 0:CT * C], AX_X, ALU.max).then_inc(s_wmax, 1)
                nc.vector.tensor_reduce(wmax[:, 3:4], ring_flat[:, 0:CT * C], AX_X, ALU.min).then_inc(s_wmax, 1)
                x_stats(0, range(CT))
                channel_aggregate("x", 0)
                dve.wait_ge(s_wall, 1)
                link(nc.vector.tensor_tensor(scale[:, :], wmax_all[:, 0:4:2], wmax_all[:, 1:4:2], ALU.max))
                link(nc.vector.tensor_scalar(inv[:, :], scale[:, :], 1e-30, 1.0 / W_TOP, ALU.max, ALU.mult))
                link(nc.vector.tensor_scalar(var_f[:, :], inv[:, 0:1], inv[:, 0:1], 1.0 / ((HD - 1) * H_UP * H_UP), ALU.mult, ALU.mult))
                link(nc.vector.tensor_scalar(var_f8[:, :], var_f[:, :], float(HD) ** -0.5, None, ALU.mult))
                link(nc.vector.tensor_scalar(proj_f[:, :], inv[:, 0:1], inv[:, 1:2], 1.0 / (H_UP * V_DOWN), ALU.mult, ALU.mult))
                nc.vector.reciprocal(scale[:, :], inv[:, :]).then_inc(s_scale, 1)
                dve.wait_ge(s_small_in, 16 * (2 + CT * FPT))
                dve.wait_ge(s_const, 3)
                link(nc.vector.tensor_scalar(offc, offc, 64.0, 4096.0, ALU.mult, ALU.min))
                link(nc.vector.tensor_scalar(offc, offc, -4096.0, None, ALU.max))
                link(nc.vector.tensor_scalar(offi, offc, RND, None, ALU.add))
                link(nc.vector.tensor_scalar(offi, offi, RND, None, ALU.subtract))
                link(nc.vector.tensor_tensor(offc, offc, offi, ALU.subtract))
                for j in range(3):
                    link(nc.vector.tensor_scalar(taps[:, :, :, j], offc, float(j - 1), None, ALU.add))
                nc.vector.tensor_tensor(taps[:, :, :, :], taps[:, :, :, :], taps[:, :, :, :], ALU.mult).then_inc(s_sub, 1)
                dve.wait_ge(s_tapexp, 1)
                for t in range(CT):
                    link(nc.vector.tensor_reduce(tsum[:, t, :], taps[:, t, :, :], AX_X, ALU.add))
                link(nc.vector.reciprocal(tsum, tsum))
                for j in range(3):
                    link(nc.vector.tensor_tensor(taps[:, :, :, j], taps[:, :, :, j], tsum, ALU.mult))
                for t in range(CT):
                    link(nc.vector.tensor_scalar(mask[:, t, :], cols, offi[:, t, 0:1], 0.0, ALU.subtract, ALU.is_ge))
                    link(nc.vector.tensor_scalar(mask2[:, t, :], cols, offi[:, t, 0:1], float(W - 1), ALU.subtract, ALU.is_le))
                link(nc.vector.tensor_tensor(mask[:, :, :], mask[:, :, :], mask2, ALU.mult))
                link(nc.vector.tensor_scalar(offr, offr, 64.0, 4096.0, ALU.mult, ALU.min))
                link(nc.vector.tensor_scalar(offr, offr, -4096.0, None, ALU.max))
                link(nc.vector.tensor_scalar(offr2, offr, RND, None, ALU.add))
                link(nc.vector.tensor_scalar(offr2, offr2, RND, None, ALU.subtract))
                link(nc.vector.tensor_scalar(offr2, offr2, float(-W), float(W), ALU.max, ALU.min))
                link(nc.vector.tensor_scalar(starts, offr2[:, :, 1], float(-W), float(MARGIN), ALU.mult, ALU.add))
                link(nc.vector.tensor_tensor(starts, starts, offr2[:, :, 0], ALU.subtract))
                nc.vector.tensor_copy(starts_i[:, :], starts).then_inc(s_starts, 1)
                nc.vector.tensor_copy(kmx1[:, :], ident[0:NH, 0:1]).then_inc(s_fin, 1)
                for u in range(WU):
                    dst, sc, t, k, r = w_unit(u)
                    cut = slice(r * 3 * P, (r + 1) * 3 * P)
                    dve.wait_ge(s_whi, u + 1)
                    nc.vector.scalar_tensor_tensor(dst[1][:, k, cut], ps[:, work_bank[u % 4], 0:3 * P], sc,
                                                   dst[0][:, k, cut], ALU.mult, ALU.subtract).then_inc(s_wlo, 1)
                group_stats_dve(dve, "x", 0, H_UP)
                for t in range(CT):
                    h_second(0, t)
                phase_a(0, None)

            def body(b):
                phase_b(b)
                group_end(b, True)
                group_stats_dve(dve, "y", b, 1.0)
                phase_a(b + 1, b)

            def last(b):
                phase_b(b)
                group_end(b, False)
                group_stats_dve(dve, "y", b, 1.0)
                for t in range(CT):
                    for part in range(3):
                        layer1_part(b, t, part)

            run(dve, first, body, last)

        @block.tensor
        def _(pe):
            def phase_a(b, room_free):
                for u in range(KU):
                    c, m = divmod(u, MT)
                    if u >= 4:
                        pe.wait_ge(s_bn, b * KU + u - 3)
                        if u - 4 < 2 * MT:
                            pe.wait_ge(s_vev, b * 2 * MT + u - 3)
                    else:
                        room_free()
                    for k in range(CT):
                        if u == 0:
                            pe.wait_ge(s_hlo, b * CT + k + 1)
                        for n, (hp, wpart) in enumerate(((0, 0), (0, 1), (1, 0))):
                            last = nc.tensor.matmul(ps[:, work_bank[u % 4], :], h_sp[:, k, hp, m * P:(m + 1) * P],
                                                    wkv[wpart][:, k, c * HALF:(c + 1) * HALF],
                                                    start=(k == 0 and n == 0), stop=(k == CT - 1 and n == 2))
                    last.then_inc(s_kv, 1)
                    if u == 18:
                        pe.wait_ge(s_av, b + 1)
                        nc.tensor.transpose(ps_at, av[:, :, :].rearrange("p h m -> p (h m)"), ident[:, :]).then_inc(s_atp, 1)
                        k_transpose(b, 0)
                    if u == 20:
                        k_spread(b, 0)

            def k_transpose(b, part):
                h0, h1 = KH[part]
                pe.wait_ge(s_kmx, b * 2 + part + 1)
                nc.tensor.transpose(ps_kt[0:h1 - h0, :], kmx[:, h0:h1], ident[:, :]).then_inc(s_ktp, 1)

            def k_spread(b, part):
                n = KH[part][1] - KH[part][0]
                pe.wait_ge(s_kdiag, b * 2 + part + 1)
                nc.tensor.matmul(ps_km[:, 0:n], ones[0:n, :], kdiag[0:n, 0:n], start=True, stop=True).then_inc(s_kmp, 1)

            def denominators(b, p):
                pe.wait_ge(s_acc, (b * NP + p + 1) * NDA)
                pe.wait_ge(s_accp, (b * NP + p + 1) * NPA)
                if p:
                    pe.wait_ge(s_dsb, b * NP + p)
                for j in (0, 1):
                    cut = slice(j * HALF, (j + 1) * HALF)
                    nc.tensor.matmul(ps[0:HD, d_bank[j], :], ones[:, 0:HD], acc[0][:, cut], start=True, stop=True)
                    nc.tensor.matmul(ps[HD:P, d_bank[j], :], ones[:, 0:HD], acc[1][:, cut], start=True, stop=False)
                    last = nc.tensor.matmul(ps[HD:P, d_bank[j], :], ones[:, 0:HD], acc_pool[:, cut], start=False, stop=True)
                last.then_inc(s_d, 1)

            def phase_b(b):
                for p in range(NP):
                    for m in range(MT):
                        i = (p * MT + m) * 2
                        pe.wait_ge(s_exp, b * NT + i + 2)
                        if m == 0 and p >= 3:
                            pe.wait_ge(s_on, b * NP + p - 2)
                        for j in (0, 1):
                            for s in (0, 1):
                                last = nc.tensor.matmul(
                                    ps[s * HD:(s + 1) * HD, o_bank[p % 3][j], :],
                                    v_sb[:, m, (2 * p + s) * HD:(2 * p + s + 1) * HD],
                                    ring[:, (i + s) % RING, j * HALF:(j + 1) * HALF],
                                    start=(m == 0), stop=(m == MT - 1))
                        last.then_inc(s_pv, 1)
                        if p and m == 0:
                            denominators(b, p - 1)
                        if p == 0 and m == 2:
                            k_transpose(b, 1)
                        if p == 0 and m == 4:
                            k_spread(b, 1)
                denominators(b, NP - 1)

            def project(b, u, ks):
                t, j = divmod(u, 2)
                for k in ks:
                    for n, (wpart, op) in enumerate(((0, 0), (1, 0), (0, 1))):
                        last = nc.tensor.matmul(ps[:, work_bank[u % 4], :], wp[wpart][:, k, t * P:(t + 1) * P],
                                                o_sp[:, k, op, j * HALF:(j + 1) * HALF],
                                                start=(k == 0 and n == 0), stop=(k == CT - 1 and n == 2))
                if k == CT - 1:
                    last.then_inc(s_pj, 1)

            def phase_c(b):
                pe.wait_ge(s_olo, b * NP + NP - 2)
                for u in range(4):
                    if u == 2:
                        pe.wait_ge(s_dsb, b * NP + NP)
                    project(b, u, range(CT - 2))
                pe.wait_ge(s_olo, b * NP + NP - 1)
                for u in range(4):
                    project(b, u, [CT - 2])
                pe.wait_ge(s_olo, b * NP + NP)
                for u in range(4):
                    project(b, u, [CT - 1])
                for u in range(4, PU):
                    pe.wait_ge(s_x1, b * PU + u - 3)
                    project(b, u, range(CT))

            def first():
                pe.wait_ge(s_ident, 2)
                pe.wait_ge(s_wkv_in, 32)
                pe.wait_ge(s_wp_in, 16)
                for u in range(WU):
                    dst, sc, nat, k, r = w_unit(u)
                    if u >= 4:
                        pe.wait_ge(s_wlo, u - 3)
                    for q in range(3):
                        last = nc.tensor.transpose(ps[:, work_bank[u % 4], q * P:(q + 1) * P],
                                                   nat[:, 3 * r + q, k * P:(k + 1) * P], ident[:, :])
                    last.then_inc(s_wt, 1)
                pe.wait_ge(s_const, 3)
                phase_a(0, lambda: pe.wait_ge(s_wlo, WU))

            def body(b):
                phase_b(b)
                phase_c(b)
                phase_a(b + 1, lambda: pe.wait_ge(s_x1, b * PU + PU))

            def last(b):
                phase_b(b)
                phase_c(b)

            run(pe, first, body, last)


_INS = ["x", "L0_conv_W_qkv", "L0_conv_W_proj", "L0_conv_b_proj", "L1_conv_offset"]


def kernel(**inputs):
    import numpy as np
    import concourse.bacc as bacc
    from concourse.bass_utils import run_bass_kernel_spmd

    nc = bacc.Bacc("TRN2", target_bir_lowering=False, num_devices=1)
    arrays, args = {}, []
    for name in _INS:
        a = np.ascontiguousarray(inputs[name])
        arrays[f"in_{name}"] = a
        args.append(nc.dram_tensor(f"in_{name}", a.shape, mybir.dt.from_np(a.dtype), kind="ExternalInput").ap())
    y = nc.dram_tensor("out", inputs["x"].shape, F32, kind="ExternalOutput").ap()
    gn_attention_displace(nc, *args, y)
    r = run_bass_kernel_spmd(nc, [arrays], core_ids=[0])
    return r.results[0]["out"]
```

```python
from contextlib import ExitStack

import concourse.bass as bass
from concourse import mybir

F32 = mybir.dt.float32
F16 = mybir.dt.float16
I32 = mybir.dt.int32
ALU = mybir.AluOpType
ACT = mybir.ActivationFunctionType
AX_X = mybir.AxisListType.X
ABSMAX = bass.bass_isa.ReduceOp.absmax

P = 128


def gn_attention_displace(nc, x, w_qkv, w_proj, b_proj, offset, out):
    B, C, H, W = x.shape
    N = H * W
    CT = C // P
    MT = N // P
    HALF = 512
    NH = 12
    HD = C // NH
    NP = NH // 2
    G = 32
    GC = C // G
    F = offset.shape[0]
    FC = C // F
    FPT = P // FC
    MARGIN = H * W + W
    ROW = N + 2 * MARGIN
    EPS = 1e-5
    KV = 2 * C
    CH = KV // HALF
    HPC = HALF // HD
    RING = 8
    H_UP = 64.0
    W_TOP = 16384.0
    V_DOWN = 2.0 ** -19
    RND = 12582912.0
    NT = NP * MT * 2
    PU = 2 * CT
    KU = CH * MT

    x_t = x.rearrange("b (t p) h w -> b p t (h w)", p=P)
    out_t = out.rearrange("b (t p) h w -> b p t (h w)", p=P)

    def scratch(name, shape, dt=F32):
        return nc.dram_tensor(name, shape, dt, kind="Internal").ap()

    a_rows = scratch("a_rows", [NH, N])
    r_rows = scratch("r_rows", [2, N])
    shift_rows = scratch("shift_rows", [C, ROW])
    cs_rows = {k: scratch(f"cs_rows_{k}", [C, 2]) for k in "xy"}
    gs_rows = {k: scratch(f"gs_rows_{k}", [C, 2]) for k in "xy"}

    ctx = ExitStack()
    with ctx:
        def sb(name, shape, dt=F32):
            return ctx.enter_context(nc.sbuf_tensor(name, shape, dt))

        def sem(name):
            return ctx.enter_context(nc.semaphore(name))

        wkv = [sb(f"wkv_{n}", [P, CT, KV], F16) for n in ("hi", "lo")]
        wp = [sb(f"wp_{n}", [P, CT, C], F16) for n in ("hi", "lo")]
        h_sp = sb("h_sp", [P, CT, 2, N], F16)
        ox = sb("ox", [P, 2 * CT * N])
        o_sp = ox[:, 0:CT * N].bitcast(F16).rearrange("p (t s n) -> p t s n", t=CT, s=2)
        x1 = ox[:, CT * N:2 * CT * N].rearrange("p (t n) -> p t n", t=CT)
        vx = sb("vx", [P, CT * N])
        v_sb = vx[:, :].rearrange("p (m c) -> p m c", m=MT)
        x_in = vx[:, :].rearrange("p (t n) -> p t n", t=CT)
        ring = sb("ring", [P, RING, N])
        a_sb = sb("a_sb", [P, 4, N])
        h32 = h_sp[:, :, :, :].rearrange("p t s n -> p (t s n)").bitcast(F32).rearrange("p (t n) -> p t n", t=CT)
        acc = ((h32[:, 0, :], h32[:, 1, :]), (h32[:, 5, :], h32[:, 1, :]))
        acc_pool = h32[:, 2, :]
        d_sb = h32[:, 3, :]
        r_sb = h32[:, 4, :]
        gn_t = [ring[:, i, :] for i in (0, 1)]
        sh_t = [ring[:, i, :] for i in (2, 3, 4)]
        tap_t = [ring[:, i, :] for i in (5, 6)]
        wkv_nat = ox[:, 0:KV // P * C].rearrange("p (r c) -> p r c", c=C)
        ring_flat = ring[:, :, :].rearrange("p r n -> p (r n)")
        wp_nat = ring_flat[:, 0:CT * C].rearrange("p (r c) -> p r c", c=C)
        zeros = ring_flat[:, 6 * N:6 * N + MARGIN]

        ident = sb("ident", [P, P])
        ones = sb("ones", [P, P])
        bias = sb("bias", [P, CT])
        taps = sb("taps", [P, CT, 2, 3])
        mask = sb("mask", [P, CT, W])
        starts_i = sb("starts_i", [1, F], I32)
        scale = sb("scale", [P, 2])
        cut_at = [0]

        def small(parts, *shape):
            n = 1
            for k in shape:
                n *= k
            v = a_sb[:, :, :].rearrange("p i n -> p (i n)")[0:parts, cut_at[0]:cut_at[0] + n]
            cut_at[0] += n
            if len(shape) == 2:
                v = v.rearrange("p (a b) -> p a b", b=shape[1])
            return v

        offc = small(P, CT, 2)
        offi = small(P, CT, 2)
        tsum = small(P, CT, 2)
        cols = small(P, W)
        mask2 = small(P, CT, W)
        offr = small(1, F, 2)
        offr2 = small(1, F, 2)
        starts = small(1, F)
        wmax = [small(P, 4), small(P, 2)]
        wmax_all = [small(P, 4), small(P, 2)]
        inv = sb("inv", [P, 2])
        var_f = sb("var_f", [P, 1])
        var_f8 = sb("var_f8", [P, 1])
        proj_f = sb("proj_f", [P, 1])
        st = sb("st", [P, MT, HPC, 6])
        dm = sb("dm", [P, MT, HPC])
        sq = sb("sq", [P, MT, HPC])
        m2 = sb("m2", [P, 2 * NH, MT])
        av = sb("av", [P, NH, MT])
        at = sb("at", [NH * MT, P])
        kmx = sb("kmx", [P, NH])
        kmx1 = sb("kmx1", [NH, 1])
        kdiag = sb("kdiag", [NH, NH])
        coef = sb("coef", [P, NH, MT])
        dt_sb = sb("dt_sb", [P, 2 * N // P])
        bst = {k: sb(f"bst_{k}", [P, CT, 2, 6]) for k in "xy"}
        mv = {k: sb(f"mv_{k}", [P, CT, 2]) for k in "xy"}
        gin = {k: sb(f"gin_{k}", [G, GC, 2]) for k in "xy"}
        gd = {k: sb(f"gd_{k}", [G, GC]) for k in "xy"}
        gq = {k: sb(f"gq_{k}", [G, GC]) for k in "xy"}
        gs = {k: sb(f"gs_{k}", [G, 6]) for k in "xy"}
        gout = {k: sb(f"gout_{k}", [G, GC, 2]) for k in "xy"}
        rb = {k: sb(f"rb_{k}", [P, CT, 2]) for k in "xy"}
        mhalf = sb("mhalf", [G, 1])

        ps = ctx.enter_context(nc.psum_tensor("ps", [P, 8, HALF], F32))
        work_bank = (0, 1, 4, 5)
        o_bank = ((0, 1), (2, 3), (6, 7))
        d_bank = (4, 5)
        ps_at = ps[0:NH * MT, 6, 0:P]
        ps_kt = ps[:, 7, 0:P]
        ps_km = ps[:, 7, P:P + NH]
        KH = ((0, 4), (4, NH))

        s_wkv_in = [sem(f"s_wkv_in{n}") for n in (0, 1)]
        s_wp_in = sem("s_wp_in")
        s_small_in = sem("s_small_in")
        s_ident = sem("s_ident")
        s_const = sem("s_const")
        s_zeros = sem("s_zeros")
        s_pads = sem("s_pads")
        s_wmax = sem("s_wmax")
        s_wall = sem("s_wall")
        s_scale = sem("s_scale")
        s_wt = sem("s_wt")
        s_whi = sem("s_whi")
        s_wlo = sem("s_wlo")
        s_sub = sem("s_sub")
        s_tapexp = sem("s_tapexp")
        s_starts = sem("s_starts")
        s_set = sem("s_set")
        s_xin = [sem(f"s_xin{t}") for t in range(CT)]
        s_bst = {k: sem(f"s_bst_{k}") for k in "xy"}
        s_stat = {k: sem(f"s_stat_{k}") for k in "xy"}
        s_cs = {k: sem(f"s_cs_{k}") for k in "xy"}
        s_gin = {k: sem(f"s_gin_{k}") for k in "xy"}
        s_gvar = {k: sem(f"s_gvar_{k}") for k in "xy"}
        s_pow = {k: sem(f"s_pow_{k}") for k in "xy"}
        s_gout = {k: sem(f"s_gout_{k}") for k in "xy"}
        s_gs = {k: sem(f"s_gs_{k}") for k in "xy"}
        s_rb = {k: sem(f"s_rb_{k}") for k in "xy"}
        s_gch = {k: sem(f"s_gch_{k}") for k in "xy"}
        s_hf = sem("s_hf")
        s_hhi = sem("s_hhi")
        s_hlo = sem("s_hlo")
        s_kv = sem("s_kv")
        s_bn = sem("s_bn")
        s_vev = sem("s_vev")
        s_ach = sem("s_ach")
        s_av = sem("s_av")
        s_atp = sem("s_atp")
        s_at = sem("s_at")
        s_arow = sem("s_arow")
        s_a = [sem(f"s_a{i}") for i in range(4)]
        s_kmx = sem("s_kmx")
        s_kch = sem("s_kch")
        s_ktp = sem("s_ktp")
        s_kdiag = sem("s_kdiag")
        s_kmp = sem("s_kmp")
        s_coef = sem("s_coef")
        s_exp = sem("s_exp")
        s_pv = sem("s_pv")
        s_acc = sem("s_acc")
        s_accp = sem("s_accp")
        s_d = sem("s_d")
        s_dsb = sem("s_dsb")
        s_dt = sem("s_dt")
        s_rt = sem("s_rt")
        s_rrow = sem("s_rrow")
        s_r = sem("s_r")
        s_on = sem("s_on")
        s_ohi = sem("s_ohi")
        s_olo = sem("s_olo")
        s_x1in = sem("s_x1in")
        s_xb = sem("s_xb")
        s_pj = sem("s_pj")
        s_x1 = sem("s_x1")
        s_gn = sem("s_gn")
        s_gst = [sem(f"s_gst{i}") for i in range(2)]
        s_sh = [sem(f"s_sh{i}") for i in range(3)]
        s_msk = sem("s_msk")
        s_tap = sem("s_tap")
        s_pch = sem("s_pch")
        s_fin = sem("s_fin")
        s_out = sem("s_out")

        s_held_sp, s_held_pool, s_held_dve = sem("s_held_sp"), sem("s_held_pool"), sem("s_held_dve")

        block = ctx.enter_context(nc.Block())

        def hold(eng, s):
            eng.sem_inc(s, 1)

        def run(eng, first, body, last):
            first()
            with eng.Fori(0, B - 1) as b:
                body(b)
            last(B - 1)

        POOL_M = 4
        DVE_ADDS = [(s, m) for m in range(1, MT) for s in (0, 1) if s == 0 or m > POOL_M]
        NDA = len(DVE_ADDS)
        NPA = POOL_M - 1

        def add_index(s, m):
            if s == 1 and m < POOL_M:
                return True, max(m, 1) - 1
            return False, DVE_ADDS.index((s, max(m, POOL_M + 1 if s else 1)))

        WU = (KV // P + CT) * CT // 3

        W_UNITS = (range(0, KV // P * CT // 3), range(KV // P * CT // 3, WU))

        def w_unit(u):
            if u < KV // P * CT // 3:
                r, k = divmod(u, CT)
                return wkv, scale[:, 0:1], wkv_nat, k, r
            r, k = divmod(u - KV // P * CT // 3, CT)
            return wp, scale[:, 1:2], wp_nat, k, r

        TAPS_AT = (6, 9, 11, 14, 16, 19)
        PCH = 4 * CT
        ACH = 5 * CH

        def group_stats_dma(sp, k, b):
            sp.wait_ge(s_stat[k], b + 1)
            sp.dma_start(cs_rows[k].rearrange("(t p) s -> p t s", p=P), mv[k][:, :, :]).then_inc(s_cs[k], 16)
            sp.wait_ge(s_cs[k], b * 16 + 16)
            sp.dma_start(gin[k][:, :, :], cs_rows[k].rearrange("(g c) s -> g c s", c=GC)).then_inc(s_gin[k], 16)
            sp.wait_ge(s_gout[k], b + 1)
            sp.dma_start(gs_rows[k].rearrange("(g c) s -> g c s", c=GC), gout[k][:, :, :]).then_inc(s_gs[k], 16)
            sp.wait_ge(s_gs[k], b * 16 + 16)
            sp.dma_start(rb[k][:, :, :], gs_rows[k].rearrange("(t p) s -> p t s", p=P)).then_inc(s_rb[k], 16)

        GCH = 6

        def group_stats_dve(dve, k, b, up):
            n = [0]

            def link(ins):
                n[0] += 1
                ins.then_inc(s_gch[k], 1)
                dve.wait_ge(s_gch[k], b * GCH + n[0])

            mean, var = gin[k][:, :, 0], gin[k][:, :, 1]
            g = gs[k]
            dve.wait_ge(s_gin[k], b * 16 + 16)
            link(nc.vector.tensor_reduce(g[:, 0:1], mean, AX_X, ALU.add))
            link(nc.vector.tensor_scalar(g[:, 1:2], g[:, 0:1], 1.0 / GC, None, ALU.mult))
            link(nc.vector.tensor_scalar(gd[k][:, :], mean, g[:, 1:2], None, ALU.subtract))
            link(nc.vector.tensor_tensor(gq[k][:, :], gd[k][:, :], gd[k][:, :], ALU.mult))
            link(nc.vector.tensor_tensor(gd[k][:, :], gq[k][:, :], var, ALU.add))
            link(nc.vector.tensor_reduce(g[:, 2:3], gd[k][:, :], AX_X, ALU.add))
            assert n[0] == GCH
            nc.vector.tensor_scalar(g[:, 3:4], g[:, 2:3], 1.0 / GC, EPS, ALU.mult, ALU.add).then_inc(s_gvar[k], 1)
            dve.wait_ge(s_pow[k], b + 1)
            nc.vector.tensor_scalar(gout[k][:, :, 0], gd[k][:, :], 0.0, g[:, 4:5], ALU.mult, ALU.add)
            nc.vector.tensor_scalar(g[:, 5:6], g[:, 1:2], g[:, 4:5], -1.0, ALU.mult, ALU.mult).then_inc(s_gvar[k], 1)
            dve.wait_ge(s_gvar[k], b * 3 + 2)
            nc.vector.tensor_scalar(gout[k][:, :, 1], gd[k][:, :], 0.0, g[:, 5:6], ALU.mult, ALU.add).then_inc(s_gvar[k], 1)
            dve.wait_ge(s_gvar[k], b * 3 + 3)
            nc.vector.tensor_scalar(gout[k][:, :, :], gout[k][:, :, :], up, None, ALU.mult).then_inc(s_gout[k], 1)

        def group_pow(pool, k, b):
            pool.wait_ge(s_gvar[k], b * 3 + 1)
            nc.gpsimd.tensor_tensor(gs[k][:, 4:5], gs[k][:, 3:4], mhalf[:, :], ALU.pow).then_inc(s_pow[k], 1)

        @block.sync
        def _(sp):
            starts_v = []

            def chain_b(b):
                for t in range(CT):
                    sp.dma_start(x1[:, t, :], x_t[b, :, t, :]).then_inc(s_x1in, 16)
                for p in range(NP):
                    for h in (2 * p + 4, 2 * p + 5):
                        if h < NH:
                            sp.wait_ge(s_exp, b * NT + 2 * MT * (p + 1))
                            sp.dma_start(a_sb[:, h % 4, :], a_rows[h:h + 1, :].broadcast_to((P, N))).then_inc(s_a[h % 4], 16)
                    sp.wait_ge(s_dsb, b * NP + p + 1)
                    for s in (0, 1):
                        sp.dma_start(dt_sb[s * P // 2:(s + 1) * P // 2, :], d_sb[s * HD:s * HD + 1, :]).then_inc(s_dt, 16)
                    sp.wait_ge(s_rt, b * NP + p + 1)
                    sp.dma_start(r_rows.rearrange("s (a n) -> (s a) n", n=2 * N // P), dt_sb[:, :]).then_inc(s_rrow, 16)
                    sp.wait_ge(s_rrow, b * NP * 16 + 16 * (p + 1))
                    if p:
                        sp.wait_ge(s_olo, b * NP + p)
                    for s in (0, 1):
                        sp.dma_start(r_sb[s * HD:(s + 1) * HD, :],
                                     r_rows[s:s + 1, :].broadcast_to((HD, N))).then_inc(s_r, 16)

            def shift_in(b, t):
                sp.wait_ge(s_gst[t % 2], b * 48 + 16 * (t // 2 + 1))
                hold(sp, s_held_sp)
                if t >= 3:
                    sp.wait_ge(s_pch, b * PCH + 4 * (t - 3) + 2)
                hold(sp, s_held_sp)
                for f in range(FPT):
                    sp.dma_start(sh_t[t % 3][f * FC:(f + 1) * FC, :],
                                 shift_rows[t * P + f * FC:t * P + (f + 1) * FC,
                                            bass.ds(start_of(t * FPT + f), N)]).then_inc(s_sh[t % 3], 16)

            def start_of(f):
                return sp.value_load(starts_i[0:1, f:f + 1], min_val=0, max_val=2 * MARGIN)

            def layer1(b):
                group_stats_dma(sp, "y", b)
                for t in range(CT + 3):
                    if t < CT:
                        sp.wait_ge(s_gn, b * CT + t + 1)
                        sp.dma_start(shift_rows[t * P:(t + 1) * P, MARGIN:MARGIN + N], gn_t[t % 2]).then_inc(s_gst[t % 2], 16)
                    if 1 <= t <= CT:
                        shift_in(b, t - 1)
                    if t >= 3:
                        sp.wait_ge(s_fin, b * CT + t - 1)
                        hold(sp, s_held_sp)
                        sp.dma_start(out_t[b, :, t - 3, :], x1[:, t - 3, :]).then_inc(s_out, 16)
                sp.wait_ge(s_out, b * CT * 16 + CT * 16)
                hold(sp, s_held_sp)

            def first():
                sp.dma_start(wkv_nat[:, 0:CT, :], w_qkv[2 * C:3 * C, :].rearrange("(r p) c -> p r c", p=P)).then_inc(s_wkv_in[0], 16)
                sp.dma_start(wkv_nat[:, CT:2 * CT, :], w_qkv[C:2 * C, :].rearrange("(r p) c -> p r c", p=P)).then_inc(s_wkv_in[1], 16)
                sp.dma_start(bias[:, :], b_proj.rearrange("(t p) -> p t", p=P), allow_slow_non_contiguous=True).then_inc(s_small_in, 16)
                sp.dma_start(offr[0:1, :, :], offset.rearrange("(a f) s -> a f s", a=1)).then_inc(s_small_in, 16)
                for t in range(CT):
                    for f in range(FPT):
                        n = t * FPT + f
                        sp.dma_start(offc[f * FC:(f + 1) * FC, t, :],
                                     offset[n:n + 1, :].broadcast_to((FC, 2))).then_inc(s_small_in, 16)
                sp.dma_start(wp_nat, w_proj.rearrange("(r p) c -> p r c", p=P)).then_inc(s_wp_in, 16)
                sp.wait_ge(s_zeros, 1)
                for t in range(CT):
                    for at_ in (0, MARGIN + N):
                        sp.dma_start(shift_rows[t * P:(t + 1) * P, at_:at_ + MARGIN], zeros).then_inc(s_pads, 16)
                group_stats_dma(sp, "x", 0)
                sp.wait_ge(s_starts, 1)
                sp.wait_ge(s_pads, 2 * CT * 16)

            def body(b):
                chain_b(b)
                group_stats_dma(sp, "x", b + 1)
                layer1(b)

            def last(b):
                chain_b(b)
                layer1(b)

            run(sp, first, body, last)

        @block.gpsimd
        def _(pool):
            def make_h(b):
                group_pow(pool, "x", b)
                pool.wait_ge(s_rb["x"], b * 16 + 16)
                hold(pool, s_held_pool)
                for t in range(CT):
                    nc.gpsimd.tensor_scalar(x_in[:, t, :], x_in[:, t, :], rb["x"][:, t, 0:1], rb["x"][:, t, 1:2],
                                            ALU.mult, ALU.add).then_inc(s_hf, 1)

            def phase_b(b):
                pool.wait_ge(s_kv, b * KU + KU)
                for p in range(NP):
                    for m in range(1, POOL_M):
                        i = p * 2 * MT + 2 * m + 1
                        pool.wait_ge(s_exp, b * NT + i + 1)
                        n = m
                        if n == 1:
                            if p:
                                pool.wait_ge(s_d, b * NP + p)
                            one = ring[:, (i - 2) % RING, :]
                        else:
                            pool.wait_ge(s_accp, (b * NP + p) * NPA + n - 1)
                            one = acc_pool
                        nc.gpsimd.tensor_tensor(acc_pool, one, ring[:, i % RING, :], ALU.add).then_inc(s_accp, 1)
                    if p > 1:
                        o_first(b, p - 2)
                    if p == 0:
                        pool.wait_ge(s_x1in, b * CT * 16 + CT * 16)
                    if p < 3:
                        hold(pool, s_held_pool)
                        for t in (2 * p, 2 * p + 1):
                            nc.gpsimd.tensor_scalar(x1[:, t, :], x1[:, t, :], 1.0, bias[:, t:t + 1],
                                                    ALU.mult, ALU.add).then_inc(s_xb, 1)

            def o_first(b, p):
                pool.wait_ge(s_on, b * NP + p + 1)
                hold(pool, s_held_pool)
                nc.gpsimd.tensor_copy(o_sp[:, p, 0, :], r_sb).then_inc(s_ohi, 1)

            def layer1(b):
                group_pow(pool, "y", b)
                pool.wait_ge(s_rb["y"], b * 16 + 16)
                hold(pool, s_held_pool)
                for t in range(CT + 3):
                    if t < CT:
                        if t >= 2:
                            pool.wait_ge(s_gst[t % 2], b * 48 + 16 * (t // 2))
                            hold(pool, s_held_pool)
                        nc.gpsimd.tensor_scalar(gn_t[t % 2], x1[:, t, :], rb["y"][:, t, 0:1], rb["y"][:, t, 1:2],
                                                ALU.mult, ALU.add).then_inc(s_gn, 1)
                    m = t - 2
                    if 0 <= m < CT:
                        sh = sh_t[m % 3].rearrange("p (y x) -> p y x", x=W)
                        pool.wait_ge(s_sh[m % 3], b * 256 + 128 * (m // 3 + 1))
                        nc.gpsimd.tensor_tensor(sh, sh, mask[:, m:m + 1, :].broadcast_to((P, H, W)),
                                                ALU.mult).then_inc(s_msk, 1)

            def first():
                nc.gpsimd.memset(zeros, 0.0).then_inc(s_zeros, 1)
                nc.gpsimd.memset(mhalf[:, :], -0.5).then_inc(s_const, 1)
                nc.gpsimd.memset(ones[:, :], 1.0).then_inc(s_const, 1)
                nc.gpsimd.memset(ident[:, :], 0.0).then_inc(s_ident, 1)
                nc.gpsimd.iota(cols, pattern=[[1, W]], base=0, channel_multiplier=0,
                               allow_small_or_imprecise_dtypes=True).then_inc(s_const, 1)
                pool.wait_ge(s_ident, 1)
                nc.gpsimd.affine_select(out=ident[:, :], in_=ident[:, :], compare_op=ALU.not_equal, fill=1.0,
                                        base=0, pattern=[[-1, P]], channel_multiplier=1).then_inc(s_ident, 1)
                pool.wait_ge(s_const, 3)
                for n in (0, 1):
                    pool.wait_ge(s_wmax, 4 + 2 * n)
                    nc.gpsimd.partition_all_reduce(wmax_all[n], wmax[n], P, ABSMAX).then_inc(s_wall, 1)
                    if n == 0:
                        make_h(0)

            def body(b):
                phase_b(b)
                make_h(b + 1)
                layer1(b)

            def last(b):
                phase_b(b)
                layer1(b)

            run(pool, first, body, last)

        @block.scalar
        def _(act):
            def make_h(b, room_free):
                for t in range(CT):
                    act.wait_ge(s_hf, b * CT + t + 1)
                    if t == 0 and room_free is not None:
                        act.wait_ge(s_ohi, room_free)
                        act.wait_ge(s_olo, room_free)
                    nc.scalar.activation(h_sp[:, t, 0, :], x_in[:, t, :], ACT.Copy).then_inc(s_hhi, 1)

            def load_x(b, tiles):
                for t in tiles:
                    act.dma_start(x_in[:, t, :], x_t[b, :, t, :]).then_inc(s_xin[t], 16)

            def phase_a(b, layer1_b):
                for u in range(KU):
                    c, m = divmod(u, MT)
                    lo, hi = c * HALF, min((c + 1) * HALF, C)
                    if lo < hi:
                        act.wait_ge(s_bn, b * KU + u + 1)
                        nc.scalar.activation(v_sb[:, m, lo:hi], ps[:, work_bank[u % 4], 0:hi - lo], ACT.Copy,
                                             scale=V_DOWN).then_inc(s_vev, 1)
                    if u == 18:
                        act.wait_ge(s_atp, b + 1)
                        nc.scalar.activation(at[:, :], ps_at, ACT.Copy).then_inc(s_at, 1)
                        act.wait_ge(s_at, b + 1)
                        act.dma_start(a_rows.rearrange("h (m n) -> (h m) n", n=P), at[:, :]).then_inc(s_arow, 16)
                        act.wait_ge(s_arow, b * 16 + 16)
                        for h in range(4):
                            act.dma_start(a_sb[:, h, :], a_rows[h:h + 1, :].broadcast_to((P, N))).then_inc(s_a[h], 16)
                    if layer1_b is not None and u + 1 in TAPS_AT:
                        middle_tap(layer1_b, TAPS_AT.index(u + 1))

            def last_o(b, p):
                act.wait_ge(s_on, b * NP + p + 1)
                nc.scalar.activation(o_sp[:, p, 0, :], r_sb, ACT.Copy).then_inc(s_ohi, 1)

            def middle_tap(b, t):
                act.wait_ge(s_msk, b * CT + t + 1)
                if t >= 2:
                    act.wait_ge(s_fin, b * CT + t)
                nc.scalar.activation(tap_t[t % 2], sh_t[t % 3], ACT.Copy,
                                     scale=taps[:, t, 1, 1:2]).then_inc(s_tap, 1)

            def phase_b(b):
                act.wait_ge(s_fin, b * CT + 1)
                for p in range(NP):
                    for m in range(MT):
                        for s in (0, 1):
                            h = 2 * p + s
                            i = (p * MT + m) * 2 + s
                            if s == 0 and m == 0 and p in (0, 2):
                                act.wait_ge(s_coef, b * 2 + p // 2 + 1)
                            if m == 0:
                                act.wait_ge(s_a[h % 4], b * 48 + 16 * (h // 4 + 1))
                            if i >= RING:
                                j = i - RING
                                pj, mj = divmod(j // 2, MT)
                                act.wait_ge(s_pv, b * (NT // 2) + j // 2 + 1)
                                by_pool, n = add_index(s, mj)
                                if by_pool:
                                    act.wait_ge(s_accp, (b * NP + pj) * NPA + n + 1)
                                else:
                                    act.wait_ge(s_acc, (b * NP + pj) * NDA + n + 1)
                            nc.scalar.activation(ring[:, i % RING, :], a_sb[:, h % 4, :], ACT.Exp,
                                                 scale=coef[:, h, m:m + 1]).then_inc(s_exp, 1)

            def weights_first(n):
                act.wait_ge(s_scale, n + 1)
                for u in W_UNITS[n]:
                    dst, sc, t, k, r = w_unit(u)
                    act.wait_ge(s_wt, u + 1)
                    nc.scalar.activation(dst[0][:, k, r * 3 * P:(r + 1) * 3 * P], ps[:, work_bank[u % 4], 0:3 * P],
                                         ACT.Copy, scale=sc).then_inc(s_whi, 1)

            def first():
                load_x(0, range(CT))
                weights_first(0)
                make_h(0, None)
                act.wait_ge(s_sub, 1)
                nc.scalar.activation(taps[:, :, :, :], taps[:, :, :, :], ACT.Exp, scale=-2.0).then_inc(s_tapexp, 1)
                weights_first(1)
                phase_a(0, None)

            def body(b):
                phase_b(b)
                act.wait_ge(s_pv, b * (NT // 2) + NT // 2)
                load_x(b + 1, range(0, CT // 2))
                last_o(b, NP - 2)
                load_x(b + 1, range(CT // 2, CT))
                last_o(b, NP - 1)
                make_h(b + 1, b * NP + NP)
                phase_a(b + 1, b)

            def last(b):
                phase_b(b)
                last_o(b, NP - 2)
                last_o(b, NP - 1)
                for t in range(CT):
                    middle_tap(b, t)

            run(act, first, body, last)

        @block.vector
        def _(dve):
            def channel_stats(k, t, halves, src):
                for j in halves:
                    nc.vector.bn_stats(bst[k][:, t, j, :], src[:, t, j * HALF:(j + 1) * HALF]).then_inc(s_bst[k], 1)

            def channel_aggregate(k, b):
                dve.wait_ge(s_bst[k], b * PU + PU)
                hold(dve, s_held_dve)
                for t in range(CT):
                    ins = nc.vector.bn_aggr(mv[k][:, t, :], bst[k][:, t, :, :].rearrange("p j s -> p (j s)"))
                ins.then_inc(s_stat[k], 1)

            def x_stats(b, tiles):
                for t in tiles:
                    dve.wait_ge(s_xin[t], b * 16 + 16)
                    channel_stats("x", t, (0, 1), x_in)

            def h_second(b, t):
                dve.wait_ge(s_hhi, b * CT + t + 1)
                nc.vector.tensor_tensor(h_sp[:, t, 1, :], x_in[:, t, :], h_sp[:, t, 0, :], ALU.subtract).then_inc(s_hlo, 1)

            def phase_a(b, layer1_b):
                n = [0]

                def link(ins, hold=True):
                    n[0] += 1
                    ins.then_inc(s_ach, 1)
                    if hold:
                        dve.wait_ge(s_ach, b * ACH + n[0])

                for u in range(KU):
                    c, m = divmod(u, MT)
                    dve.wait_ge(s_kv, b * KU + u + 1)
                    for g in range(HPC):
                        ins = nc.vector.bn_stats(st[:, m, g, :], ps[:, work_bank[u % 4], g * HD:(g + 1) * HD])
                    ins.then_inc(s_bn, 1)
                    if m == MT - 1:
                        dve.wait_ge(s_bn, b * KU + u + 1)
                        dst = m2[:, c * HPC:(c + 1) * HPC, :].rearrange("p g m -> p m g")
                        link(nc.vector.tensor_tensor(dm[:, :, :], st[:, :, :, 1], st[:, :, :, 4], ALU.subtract))
                        link(nc.vector.tensor_tensor(sq[:, :, :], dm[:, :, :], dm[:, :, :], ALU.mult))
                        link(nc.vector.tensor_tensor(dm[:, :, :], st[:, :, :, 2], st[:, :, :, 5], ALU.add))
                        link(nc.vector.tensor_scalar(sq[:, :, :], sq[:, :, :], HD / 4.0, None, ALU.mult))
                        link(nc.vector.tensor_tensor(dst, sq[:, :, :], dm[:, :, :], ALU.add))
                    if u == 2 * MT - 1:
                        nc.vector.tensor_scalar(av[:, :, :], m2[:, 0:NH, :], var_f[:, 0:1], None, ALU.mult).then_inc(s_av, 1)
                        k_partition_max(0)
                    if u == 19:
                        k_max(b, 0)
                    if u == 21:
                        k_scales(b, 0)
                    if layer1_b is not None and u in TAPS_AT:
                        taps_y(layer1_b, TAPS_AT.index(u))
                    if layer1_b is not None and u - 1 in TAPS_AT:
                        taps_x(layer1_b, TAPS_AT.index(u - 1))
                k_partition_max(1)
                assert n[0] == ACH

            def k_partition_max(part):
                h0, h1 = KH[part]
                nc.vector.tensor_reduce(kmx[:, h0:h1], m2[:, NH + h0:NH + h1, :], AX_X, ALU.max).then_inc(s_kmx, 1)

            def k_max(b, part):
                h0, h1 = KH[part]
                dve.wait_ge(s_ktp, b * 2 + part + 1)
                nc.vector.tensor_reduce(kmx1[0:h1 - h0, :], ps_kt[0:h1 - h0, :], AX_X, ALU.max).then_inc(s_kch, 1)
                dve.wait_ge(s_kch, b * 4 + 2 * part + 1)
                nc.vector.tensor_scalar(kdiag[0:h1 - h0, 0:h1 - h0], ident[0:h1 - h0, 0:h1 - h0], kmx1[0:h1 - h0, 0:1],
                                        None, ALU.mult).then_inc(s_kdiag, 1)

            def k_scales(b, part):
                h0, h1 = KH[part]
                dve.wait_ge(s_kmp, b * 2 + part + 1)
                nc.vector.tensor_tensor(coef[:, h0:h1, :], m2[:, NH + h0:NH + h1, :],
                                        ps_km[:, 0:h1 - h0].unsqueeze(2).broadcast_to((P, h1 - h0, MT)),
                                        ALU.subtract).then_inc(s_kch, 1)
                dve.wait_ge(s_kch, b * 4 + 2 * part + 2)
                nc.vector.tensor_scalar(coef[:, h0:h1, :], coef[:, h0:h1, :], var_f8[:, 0:1], 0.0,
                                        ALU.mult, ALU.min).then_inc(s_coef, 1)

            def add_tap(b, t, n, out_, in_, k):
                nc.vector.scalar_tensor_tensor(out_, in_, k, out_, ALU.mult, ALU.add).then_inc(s_pch, 1)
                dve.wait_ge(s_pch, b * PCH + 4 * t + n)

            def taps_y(b, t):
                sh = sh_t[t % 3].rearrange("p (y x) -> p y x", x=W)
                tp = tap_t[t % 2].rearrange("p (y x) -> p y x", x=W)
                ky = taps[:, t, 1, :]
                dve.wait_ge(s_tap, b * CT + t + 1)
                add_tap(b, t, 1, tp[:, 1:H, :], sh[:, 0:H - 1, :], ky[:, 0:1])
                add_tap(b, t, 2, tp[:, 0:H - 1, :], sh[:, 1:H, :], ky[:, 2:3])

            def taps_x(b, t):
                tp = tap_t[t % 2].rearrange("p (y x) -> p y x", x=W)
                xt = x1[:, t, :].rearrange("p (y x) -> p y x", x=W)
                kx = taps[:, t, 0, :]
                add_tap(b, t, 3, xt, tp, kx[:, 1:2])
                add_tap(b, t, 4, xt[:, :, 1:W], tp[:, :, 0:W - 1], kx[:, 0:1])
                nc.vector.scalar_tensor_tensor(xt[:, :, 0:W - 1], tp[:, :, 1:W], kx[:, 2:3], xt[:, :, 0:W - 1],
                                               ALU.mult, ALU.add).then_inc(s_fin, 1)

            def d_copy(b, p):
                dve.wait_ge(s_d, b * NP + p + 1)
                if p:
                    dve.wait_ge(s_dt, b * NP * 32 + 32 * p)
                nc.vector.tensor_copy(d_sb.rearrange("p (a n) -> p a n", a=2), ps[:, 4:6, :]).then_inc(s_dsb, 1)

            def d_reciprocal(b, p):
                dve.wait_ge(s_dt, b * NP * 32 + 32 * (p + 1))
                nc.vector.reciprocal(dt_sb[:, :], dt_sb[:, :]).then_inc(s_rt, 1)

            def o_normalise(b, p):
                dve.wait_ge(s_r, b * NP * 32 + 32 * (p + 1))
                r2 = r_sb.rearrange("p (a n) -> p a n", a=2)
                k = o_bank[p % 3][0]
                nc.vector.tensor_tensor(r2, ps[:, k:k + 2, :], r2, ALU.mult).then_inc(s_on, 1)

            def o_second(b, p):
                dve.wait_ge(s_ohi, b * NP + p + 1)
                nc.vector.tensor_tensor(o_sp[:, p, 1, :], r_sb, o_sp[:, p, 0, :], ALU.subtract).then_inc(s_olo, 1)

            def phase_b(b):
                for p in range(NP):
                    done = (b * NP + p) * NDA
                    for n, (s, m) in enumerate(DVE_ADDS):
                        i = (p * MT + m) * 2 + s
                        dve.wait_ge(s_exp, b * NT + i + 1)
                        if m == (POOL_M + 1 if s else 1):
                            if p and s == 1:
                                dve.wait_ge(s_d, b * NP + p)
                            one = ring[:, (i - 2) % RING, :]
                        else:
                            dve.wait_ge(s_acc, done + add_index(s, m - 1)[1] + 1)
                            one = acc[p % 2][s]
                        nc.vector.tensor_tensor(acc[p % 2][s], one, ring[:, i % RING, :], ALU.add).then_inc(s_acc, 1)
                        if p == 0 and (s, m) == (0, 3):
                            k_max(b, 1)
                        if p == 0 and (s, m) == (0, 6):
                            k_scales(b, 1)
                        if p and (s, m) == (0, 3):
                            d_copy(b, p - 1)
                        if p > 1 and (s, m) == (0, 4):
                            o_normalise(b, p - 2)
                        if p and (s, m) == (0, 6):
                            d_reciprocal(b, p - 1)
                        if p > 2 and (s, m) == (0, 1):
                            o_second(b, p - 3)

            def group_end(b, with_next):
                o_second(b, NP - 3)
                d_copy(b, NP - 1)
                o_normalise(b, NP - 2)
                o_second(b, NP - 2)
                d_reciprocal(b, NP - 1)
                if with_next:
                    x_stats(b + 1, range(0, 6))
                    channel_aggregate("x", b + 1)
                o_normalise(b, NP - 1)
                o_second(b, NP - 1)
                for u in range(PU):
                    t, j = divmod(u, 2)
                    if u == 2 and with_next:
                        group_stats_dve(dve, "x", b + 1, H_UP)
                    dve.wait_ge(s_pj, b * PU + u + 1)
                    if u == 0:
                        dve.wait_ge(s_xb, b * CT + CT)
                    cut = x1[:, t, j * HALF:(j + 1) * HALF]
                    nc.vector.scalar_tensor_tensor(cut, ps[:, work_bank[u % 4], :], proj_f[:, 0:1], cut,
                                                   ALU.mult, ALU.add).then_inc(s_x1, 1)
                    if with_next and 4 <= u < 4 + CT:
                        h_second(b + 1, u - 4)
                    dve.wait_ge(s_x1, b * PU + u + 1)
                    channel_stats("y", t, (j,), x1)
                channel_aggregate("y", b)

            def first():
                n = [0]

                def link(ins):
                    n[0] += 1
                    ins.then_inc(s_set, 1)
                    dve.wait_ge(s_set, n[0])

                def weights_range(dst, src):
                    nc.vector.tensor_reduce(dst[:, 0:1], src, AX_X, ALU.max).then_inc(s_wmax, 1)
                    nc.vector.tensor_reduce(dst[:, 1:2], src, AX_X, ALU.min).then_inc(s_wmax, 1)

                def weights_second(k):
                    for u in W_UNITS[k]:
                        dst, sc, t, kt, r = w_unit(u)
                        cut = slice(r * 3 * P, (r + 1) * 3 * P)
                        dve.wait_ge(s_whi, u + 1)
                        nc.vector.scalar_tensor_tensor(dst[1][:, kt, cut], ps[:, work_bank[u % 4], 0:3 * P], sc,
                                                       dst[0][:, kt, cut], ALU.mult, ALU.subtract).then_inc(s_wlo, 1)

                def weights_scale(k):
                    dve.wait_ge(s_wall, k + 1)
                    link(nc.vector.tensor_reduce(inv[:, k:k + 1], wmax_all[k], AX_X, ALU.max))
                    link(nc.vector.tensor_scalar(inv[:, k:k + 1], inv[:, k:k + 1], 1e-30, 1.0 / W_TOP, ALU.max, ALU.mult))
                    nc.vector.reciprocal(scale[:, k:k + 1], inv[:, k:k + 1]).then_inc(s_scale, 1)
                    dve.wait_ge(s_scale, k + 1)

                for part in (0, 1):
                    dve.wait_ge(s_wkv_in[part], 16)
                    weights_range(wmax[0][:, 2 * part:2 * part + 2], ox[:, part * CT * C:(part + 1) * CT * C])
                x_stats(0, range(CT))
                channel_aggregate("x", 0)
                weights_scale(0)
                link(nc.vector.tensor_scalar(var_f[:, :], inv[:, 0:1], inv[:, 0:1], 1.0 / ((HD - 1) * H_UP * H_UP), ALU.mult, ALU.mult))
                link(nc.vector.tensor_scalar(var_f8[:, :], var_f[:, :], float(HD) ** -0.5, None, ALU.mult))
                weights_second(0)
                group_stats_dve(dve, "x", 0, H_UP)
                dve.wait_ge(s_wp_in, 16)
                weights_range(wmax[1], ring_flat[:, 0:CT * C])
                for t in range(CT):
                    h_second(0, t)
                dve.wait_ge(s_small_in, 16 * (2 + CT * FPT))
                dve.wait_ge(s_const, 3)
                link(nc.vector.tensor_scalar(offc, offc, 64.0, 4096.0, ALU.mult, ALU.min))
                link(nc.vector.tensor_scalar(offc, offc, -4096.0, None, ALU.max))
                link(nc.vector.tensor_scalar(offi, offc, RND, None, ALU.add))
                link(nc.vector.tensor_scalar(offi, offi, RND, None, ALU.subtract))
                link(nc.vector.tensor_tensor(offc, offc, offi, ALU.subtract))
                for j in range(3):
                    link(nc.vector.tensor_scalar(taps[:, :, :, j], offc, float(j - 1), None, ALU.add))
                nc.vector.tensor_tensor(taps[:, :, :, :], taps[:, :, :, :], taps[:, :, :, :], ALU.mult).then_inc(s_sub, 1)
                weights_scale(1)
                link(nc.vector.tensor_scalar(proj_f[:, :], inv[:, 0:1], inv[:, 1:2], 1.0 / (H_UP * V_DOWN), ALU.mult, ALU.mult))
                weights_second(1)
                dve.wait_ge(s_tapexp, 1)
                for t in range(CT):
                    link(nc.vector.tensor_reduce(tsum[:, t, :], taps[:, t, :, :], AX_X, ALU.add))
                link(nc.vector.reciprocal(tsum, tsum))
                for j in range(3):
                    link(nc.vector.tensor_tensor(taps[:, :, :, j], taps[:, :, :, j], tsum, ALU.mult))
                for t in range(CT):
                    link(nc.vector.tensor_scalar(mask[:, t, :], cols, offi[:, t, 0:1], 0.0, ALU.subtract, ALU.is_ge))
                    link(nc.vector.tensor_scalar(mask2[:, t, :], cols, offi[:, t, 0:1], float(W - 1), ALU.subtract, ALU.is_le))
                link(nc.vector.tensor_tensor(mask[:, :, :], mask[:, :, :], mask2, ALU.mult))
                link(nc.vector.tensor_scalar(offr, offr, 64.0, 4096.0, ALU.mult, ALU.min))
                link(nc.vector.tensor_scalar(offr, offr, -4096.0, None, ALU.max))
                link(nc.vector.tensor_scalar(offr2, offr, RND, None, ALU.add))
                link(nc.vector.tensor_scalar(offr2, offr2, RND, None, ALU.subtract))
                link(nc.vector.tensor_scalar(offr2, offr2, float(-W), float(W), ALU.max, ALU.min))
                link(nc.vector.tensor_scalar(starts, offr2[:, :, 1], float(-W), float(MARGIN), ALU.mult, ALU.add))
                link(nc.vector.tensor_tensor(starts, starts, offr2[:, :, 0], ALU.subtract))
                nc.vector.tensor_copy(starts_i[:, :], starts).then_inc(s_starts, 1)
                nc.vector.tensor_copy(kmx1[:, :], ident[0:NH, 0:1]).then_inc(s_fin, 1)
                phase_a(0, None)

            def body(b):
                phase_b(b)
                group_end(b, True)
                group_stats_dve(dve, "y", b, 1.0)
                phase_a(b + 1, b)

            def last(b):
                phase_b(b)
                group_end(b, False)
                group_stats_dve(dve, "y", b, 1.0)
                for t in range(CT):
                    taps_y(b, t)
                    taps_x(b, t)

            run(dve, first, body, last)

        @block.tensor
        def _(pe):
            def phase_a(b, room_free):
                for u in range(KU):
                    c, m = divmod(u, MT)
                    if u >= 4:
                        pe.wait_ge(s_bn, b * KU + u - 3)
                        if u - 4 < 2 * MT:
                            pe.wait_ge(s_vev, b * 2 * MT + u - 3)
                    else:
                        room_free()
                    for k in range(CT):
                        if u == 0:
                            pe.wait_ge(s_hlo, b * CT + k + 1)
                        for n, (hp, wpart) in enumerate(((0, 0), (0, 1), (1, 0))):
                            last = nc.tensor.matmul(ps[:, work_bank[u % 4], :], h_sp[:, k, hp, m * P:(m + 1) * P],
                                                    wkv[wpart][:, k, c * HALF:(c + 1) * HALF],
                                                    start=(k == 0 and n == 0), stop=(k == CT - 1 and n == 2))
                    last.then_inc(s_kv, 1)
                    if u == 18:
                        pe.wait_ge(s_av, b + 1)
                        nc.tensor.transpose(ps_at, av[:, :, :].rearrange("p h m -> p (h m)"), ident[:, :]).then_inc(s_atp, 1)
                        k_transpose(b, 0)
                    if u == 20:
                        k_spread(b, 0)

            def k_transpose(b, part):
                h0, h1 = KH[part]
                pe.wait_ge(s_kmx, b * 2 + part + 1)
                nc.tensor.transpose(ps_kt[0:h1 - h0, :], kmx[:, h0:h1], ident[:, :]).then_inc(s_ktp, 1)

            def k_spread(b, part):
                n = KH[part][1] - KH[part][0]
                pe.wait_ge(s_kdiag, b * 2 + part + 1)
                nc.tensor.matmul(ps_km[:, 0:n], ones[0:n, :], kdiag[0:n, 0:n], start=True, stop=True).then_inc(s_kmp, 1)

            def denominators(b, p):
                pe.wait_ge(s_acc, (b * NP + p + 1) * NDA)
                pe.wait_ge(s_accp, (b * NP + p + 1) * NPA)
                if p:
                    pe.wait_ge(s_dsb, b * NP + p)
                for j in (0, 1):
                    cut = slice(j * HALF, (j + 1) * HALF)
                    nc.tensor.matmul(ps[0:HD, d_bank[j], :], ones[:, 0:HD], acc[p % 2][0][:, cut], start=True, stop=True)
                    nc.tensor.matmul(ps[HD:P, d_bank[j], :], ones[:, 0:HD], acc[p % 2][1][:, cut], start=True, stop=False)
                    last = nc.tensor.matmul(ps[HD:P, d_bank[j], :], ones[:, 0:HD], acc_pool[:, cut], start=False, stop=True)
                last.then_inc(s_d, 1)

            def phase_b(b):
                for p in range(NP):
                    for m in range(MT):
                        i = (p * MT + m) * 2
                        pe.wait_ge(s_exp, b * NT + i + 2)
                        if m == 0 and p >= 3:
                            pe.wait_ge(s_on, b * NP + p - 2)
                        for j in (0, 1):
                            for s in (0, 1):
                                last = nc.tensor.matmul(
                                    ps[s * HD:(s + 1) * HD, o_bank[p % 3][j], :],
                                    v_sb[:, m, (2 * p + s) * HD:(2 * p + s + 1) * HD],
                                    ring[:, (i + s) % RING, j * HALF:(j + 1) * HALF],
                                    start=(m == 0), stop=(m == MT - 1))
                        last.then_inc(s_pv, 1)
                        if p and m == 0:
                            denominators(b, p - 1)
                        if p == 0 and m == 2:
                            k_transpose(b, 1)
                        if p == 0 and m == 4:
                            k_spread(b, 1)
                denominators(b, NP - 1)

            def project(b, u, ks):
                t, j = divmod(u, 2)
                for k in ks:
                    for n, (wpart, op) in enumerate(((0, 0), (1, 0), (0, 1))):
                        last = nc.tensor.matmul(ps[:, work_bank[u % 4], :], wp[wpart][:, k, t * P:(t + 1) * P],
                                                o_sp[:, k, op, j * HALF:(j + 1) * HALF],
                                                start=(k == 0 and n == 0), stop=(k == CT - 1 and n == 2))
                if k == CT - 1:
                    last.then_inc(s_pj, 1)

            def phase_c(b):
                pe.wait_ge(s_olo, b * NP + NP - 2)
                for u in range(4):
                    if u == 2:
                        pe.wait_ge(s_dsb, b * NP + NP)
                    project(b, u, range(CT - 2))
                pe.wait_ge(s_olo, b * NP + NP - 1)
                for u in range(4):
                    project(b, u, [CT - 2])
                pe.wait_ge(s_olo, b * NP + NP)
                for u in range(4):
                    project(b, u, [CT - 1])
                for u in range(4, PU):
                    pe.wait_ge(s_x1, b * PU + u - 3)
                    project(b, u, range(CT))

            def first():
                pe.wait_ge(s_ident, 2)
                for u in range(WU):
                    dst, sc, nat, k, r = w_unit(u)
                    if u in (0, W_UNITS[0][-1] // 2 + 1):
                        pe.wait_ge(s_wkv_in[1 if u else 0], 16)
                    if u == W_UNITS[1][0]:
                        pe.wait_ge(s_wp_in, 16)
                    if u >= 4:
                        pe.wait_ge(s_wlo, u - 3)
                    for q in range(3):
                        last = nc.tensor.transpose(ps[:, work_bank[u % 4], q * P:(q + 1) * P],
                                                   nat[:, 3 * r + q, k * P:(k + 1) * P], ident[:, :])
                    last.then_inc(s_wt, 1)
                pe.wait_ge(s_const, 3)
                phase_a(0, lambda: pe.wait_ge(s_wlo, WU))

            def body(b):
                phase_b(b)
                phase_c(b)
                phase_a(b + 1, lambda: pe.wait_ge(s_x1, b * PU + PU))

            def last(b):
                phase_b(b)
                phase_c(b)

            run(pe, first, body, last)


_INS = ["x", "L0_conv_W_qkv", "L0_conv_W_proj", "L0_conv_b_proj", "L1_conv_offset"]


def kernel(**inputs):
    import numpy as np
    import concourse.bacc as bacc
    from concourse.bass_utils import run_bass_kernel_spmd

    nc = bacc.Bacc("TRN2", target_bir_lowering=False, num_devices=1)
    arrays, args = {}, []
    for name in _INS:
        a = np.ascontiguousarray(inputs[name])
        arrays[f"in_{name}"] = a
        args.append(nc.dram_tensor(f"in_{name}", a.shape, mybir.dt.from_np(a.dtype), kind="ExternalInput").ap())
    y = nc.dram_tensor("out", inputs["x"].shape, F32, kind="ExternalOutput").ap()
    gn_attention_displace(nc, *args, y)
    r = run_bass_kernel_spmd(nc, [arrays], core_ids=[0])
    return r.results[0]["out"]
```

```python
from contextlib import ExitStack

import concourse.bass as bass
from concourse import mybir

F32 = mybir.dt.float32
F16 = mybir.dt.float16
BF16 = mybir.dt.bfloat16
I32 = mybir.dt.int32
ALU = mybir.AluOpType
ACT = mybir.ActivationFunctionType
AX_X = mybir.AxisListType.X
ABSMAX = bass.bass_isa.ReduceOp.absmax

P = 128


def gn_attention_displace(nc, x, w_qkv, w_proj, b_proj, offset, out):
    B, C, H, W = x.shape
    N = H * W
    CT = C // P
    MT = N // P
    HALF = 512
    NH = 12
    HD = C // NH
    NP = NH // 2
    G = 32
    GC = C // G
    F = offset.shape[0]
    FC = C // F
    FPT = P // FC
    MARGIN = H * W + W
    ROW = N + 2 * MARGIN
    EPS = 1e-5
    KV = 2 * C
    CH = KV // HALF
    HPC = HALF // HD
    RING = 10
    H_UP = 64.0
    W_TOP = 16384.0
    V_DOWN = 2.0 ** -19
    RND = 12582912.0
    NR = NP - 1
    NT = NP * MT * 2
    PU = 2 * CT
    KU = CH * MT

    x_t = x.rearrange("b (t p) h w -> b p t (h w)", p=P)
    out_t = out.rearrange("b (t p) h w -> b p t (h w)", p=P)

    def scratch(name, shape, dt=F32):
        return nc.dram_tensor(name, shape, dt, kind="Internal").ap()

    a_rows = scratch("a_rows", [NH, N])
    r_rows = scratch("r_rows", [2, N])
    shift_rows = scratch("shift_rows", [C, ROW])
    cs_rows = {k: scratch(f"cs_rows_{k}", [C, 2]) for k in "xy"}
    gs_rows = {k: scratch(f"gs_rows_{k}", [C, 2]) for k in "xy"}

    ctx = ExitStack()
    with ctx:
        def sb(name, shape, dt=F32):
            return ctx.enter_context(nc.sbuf_tensor(name, shape, dt))

        def sem(name):
            return ctx.enter_context(nc.semaphore(name))

        wkv = [sb(f"wkv_{n}", [P, CT, KV], F16) for n in ("hi", "lo")]
        wp = [sb(f"wp_{n}", [P, CT, C], F16) for n in ("hi", "lo")]
        h_sp = sb("h_sp", [P, CT, 2, N], F16)
        ox = sb("ox", [P, 2 * CT * N])
        o_sp = ox[:, 0:CT * N].bitcast(F16).rearrange("p (t s n) -> p t s n", t=CT, s=2)
        x1 = ox[:, CT * N:2 * CT * N].rearrange("p (t n) -> p t n", t=CT)
        vx = sb("vx", [P, CT * N])
        v_sb = vx[:, :].rearrange("p (m c) -> p m c", m=MT)
        x_in = vx[:, :].rearrange("p (t n) -> p t n", t=CT)
        ring = sb("ring", [P, RING - 2, N])
        ring_t = [ring[:, i, :] for i in range(RING - 2)] + [ox[:, i * N:(i + 1) * N] for i in (CT - 2, CT - 1)]
        a_sb = sb("a_sb", [P, 4, N])
        h32 = h_sp[:, :, :, :].rearrange("p t s n -> p (t s n)").bitcast(F32).rearrange("p (t n) -> p t n", t=CT)
        acc = ((h32[:, 0, :], h32[:, 1, :]), (h32[:, 5, :], h32[:, 1, :]))
        acc_pool = h32[:, 2, :]
        d_sb = h32[:, 3, :]
        r_of = [h32[:, 4, :]] * (NP - 2) + [a_sb[:, 0, :], a_sb[:, 1, :]]
        gn_t = [ring_t[RING - 2], ring_t[RING - 1]]
        sh_t = [ring_t[RING - 3]] + [ox[:, i * N:(i + 1) * N] for i in (0, 1)]
        tap_t = [ox[:, i * N:(i + 1) * N] for i in (2, 3)]
        wkv_nat = ox[:, 0:KV // P * C].rearrange("p (r c) -> p r c", c=C)
        ring_flat = ring[:, :, :].rearrange("p r n -> p (r n)")
        wp_nat = ring_flat[:, 0:CT * C].rearrange("p (r c) -> p r c", c=C)
        zeros = ring_flat[:, 5 * N:5 * N + MARGIN]

        ident = sb("ident", [P, P])
        ones = sb("ones", [P, P])
        bias = sb("bias", [P, CT])
        taps = sb("taps", [P, CT, 2, 3])
        mask = sb("mask", [P, CT, W])
        starts_i = sb("starts_i", [1, F], I32)
        scale = sb("scale", [P, 2])
        cut_at = [(RING - 3) * N]

        def small(parts, *shape):
            n = 1
            for k in shape:
                n *= k
            v = ring_flat[0:parts, cut_at[0]:cut_at[0] + n]
            cut_at[0] += n
            if len(shape) == 2:
                v = v.rearrange("p (a b) -> p a b", b=shape[1])
            return v

        offc = small(P, CT, 2)
        offi = small(P, CT, 2)
        tsum = small(P, CT, 2)
        cols = small(P, W)
        mask2 = small(P, CT, W)
        offr = small(1, F, 2)
        offr2 = small(1, F, 2)
        starts = small(1, F)
        wmax = [small(P, 4), small(P, 1)]
        wmax_all = [small(P, 4), small(P, 1)]
        assert cut_at[0] <= (RING - 2) * N
        wkv_abs = wkv[0][:, :, :].rearrange("p t c -> p (t c)").bitcast(BF16)
        wp_abs = wp[0][:, :, :].rearrange("p t c -> p (t c)").bitcast(BF16)
        inv = sb("inv", [P, 2])
        var_f = sb("var_f", [P, 1])
        var_f8 = sb("var_f8", [P, 1])
        proj_f = sb("proj_f", [P, 1])
        st = sb("st", [P, MT, HPC, 6])
        dm = sb("dm", [P, MT, HPC])
        sq = sb("sq", [P, MT, HPC])
        m2 = sb("m2", [P, 2 * NH, MT])
        av = sb("av", [P, NH, MT])
        at = sb("at", [NH * MT, P])
        kmx = sb("kmx", [P, NH])
        kmx1 = sb("kmx1", [NH, 1])
        kdiag = sb("kdiag", [NH, NH])
        coef = sb("coef", [P, NH, MT])
        dt_sb = sb("dt_sb", [P, 2 * N // P])
        bst = {k: sb(f"bst_{k}", [P, CT, 2, 6]) for k in "xy"}
        mv = {k: sb(f"mv_{k}", [P, CT, 2]) for k in "xy"}
        gin = {k: sb(f"gin_{k}", [G, GC, 2]) for k in "xy"}
        gd = {k: sb(f"gd_{k}", [G, GC]) for k in "xy"}
        gq = {k: sb(f"gq_{k}", [G, GC]) for k in "xy"}
        gs = {k: sb(f"gs_{k}", [G, 6]) for k in "xy"}
        gout = {k: sb(f"gout_{k}", [G, GC, 2]) for k in "xy"}
        rb = {k: sb(f"rb_{k}", [P, CT, 2]) for k in "xy"}
        mhalf = sb("mhalf", [G, 1])

        ps = ctx.enter_context(nc.psum_tensor("ps", [P, 8, HALF], F32))
        kv_bank = (0, 1, 4, 5)
        pj_bank = (2, 3, 4, 5)
        o_bank = ((2, 3), (0, 1), (6, 7))
        d_bank = (4, 5)
        ps_at = ps[0:NH * MT, 6, 0:P]
        ps_kt = ps[:, 7, 0:P]
        ps_km = ps[:, 7, P:P + NH]
        KH = ((0, 4), (4, NH))

        s_wkv_in = [sem(f"s_wkv_in{n}") for n in range(4)]
        s_wp_in = sem("s_wp_in")
        s_small_in = sem("s_small_in")
        s_ident = sem("s_ident")
        s_const = sem("s_const")
        s_zeros = sem("s_zeros")
        s_pads = sem("s_pads")
        s_wabs = sem("s_wabs")
        s_wmax = sem("s_wmax")
        s_wall = sem("s_wall")
        s_scale = sem("s_scale")
        s_wt = sem("s_wt")
        s_whi = sem("s_whi")
        s_wlo = sem("s_wlo")
        s_sub = sem("s_sub")
        s_tapexp = sem("s_tapexp")
        s_starts = sem("s_starts")
        s_set = sem("s_set")
        s_xin = [sem(f"s_xin{t}") for t in range(CT)]
        s_bst = {k: sem(f"s_bst_{k}") for k in "xy"}
        s_stat = {k: sem(f"s_stat_{k}") for k in "xy"}
        s_cs = {k: sem(f"s_cs_{k}") for k in "xy"}
        s_gin = {k: sem(f"s_gin_{k}") for k in "xy"}
        s_gvar = {k: sem(f"s_gvar_{k}") for k in "xy"}
        s_pow = {k: sem(f"s_pow_{k}") for k in "xy"}
        s_gout = {k: sem(f"s_gout_{k}") for k in "xy"}
        s_gs = {k: sem(f"s_gs_{k}") for k in "xy"}
        s_rb = {k: sem(f"s_rb_{k}") for k in "xy"}
        s_gch = {k: sem(f"s_gch_{k}") for k in "xy"}
        s_hf = sem("s_hf")
        s_hhi = sem("s_hhi")
        s_hlo = sem("s_hlo")
        s_kv = sem("s_kv")
        s_bn = sem("s_bn")
        s_vev = sem("s_vev")
        s_ach = sem("s_ach")
        s_av = sem("s_av")
        s_atp = sem("s_atp")
        s_at = sem("s_at")
        s_arow = sem("s_arow")
        s_a = [sem(f"s_a{i}") for i in range(4)]
        s_kmx = sem("s_kmx")
        s_kch = sem("s_kch")
        s_ktp = sem("s_ktp")
        s_kdiag = sem("s_kdiag")
        s_kmp = sem("s_kmp")
        s_coef = sem("s_coef")
        s_exp = sem("s_exp")
        s_pv = sem("s_pv")
        s_acc = sem("s_acc")
        s_accp = sem("s_accp")
        s_d = sem("s_d")
        s_dsb = sem("s_dsb")
        s_rlast = sem("s_rlast")
        s_dt = sem("s_dt")
        s_rt = sem("s_rt")
        s_rrow = sem("s_rrow")
        s_r = sem("s_r")
        s_on = sem("s_on")
        s_ohi = sem("s_ohi")
        s_olo = sem("s_olo")
        s_x1in = sem("s_x1in")
        s_xb = sem("s_xb")
        s_pj = sem("s_pj")
        s_x1 = sem("s_x1")
        s_gn = sem("s_gn")
        s_gst = [sem(f"s_gst{i}") for i in range(2)]
        s_sh = [sem(f"s_sh{i}") for i in range(3)]
        s_msk = sem("s_msk")
        s_tap = sem("s_tap")
        s_pch = sem("s_pch")
        s_fin = sem("s_fin")
        s_out = sem("s_out")

        s_held_sp, s_held_pool, s_held_dve = sem("s_held_sp"), sem("s_held_pool"), sem("s_held_dve")

        block = ctx.enter_context(nc.Block())

        def hold(eng, s):
            eng.sem_inc(s, 1)

        def run(eng, first, body, last):
            first()
            with eng.Fori(0, B - 1) as b:
                body(b)
            last(B - 1)

        POOL_M = 5
        DVE_ADDS = [(0, m) for m in range(1, POOL_M)] + [(s, m) for m in range(POOL_M, MT) for s in (0, 1)]
        NDA = len(DVE_ADDS)
        NPA = POOL_M - 1

        def add_index(s, m):
            if s == 1 and m < POOL_M:
                return True, max(m, 1) - 1
            return False, DVE_ADDS.index((s, max(m, 1)))

        WU = (KV // P + CT) * CT // 3

        WKU = KV // P * CT // 3
        QUARTER = KV // P * C // 4

        def w_unit(u):
            if u < WKU:
                r, k = divmod(u, CT)
                return wkv, scale[:, 0:1], wkv_nat, k, r, ps[:, kv_bank[u % 4], 0:3 * P]
            r, k = divmod(u - WKU, CT)
            return wp, scale[:, 1:2], wp_nat, k, r, ps[:, 2 + u % 2, 0:3 * P]

        TAPS_AT = (7, 9, 11, 14, 16, 19)
        AT_AT = 18
        PCH = 4 * CT
        ACH = 5 * CH

        def group_stats_dma(sp, k, b):
            sp.wait_ge(s_stat[k], b + 1)
            sp.dma_start(cs_rows[k].rearrange("(t p) s -> p t s", p=P), mv[k][:, :, :]).then_inc(s_cs[k], 16)
            sp.wait_ge(s_cs[k], b * 16 + 16)
            sp.dma_start(gin[k][:, :, :], cs_rows[k].rearrange("(g c) s -> g c s", c=GC)).then_inc(s_gin[k], 16)
            sp.wait_ge(s_gout[k], b + 1)
            sp.dma_start(gs_rows[k].rearrange("(g c) s -> g c s", c=GC), gout[k][:, :, :]).then_inc(s_gs[k], 16)
            sp.wait_ge(s_gs[k], b * 16 + 16)
            sp.dma_start(rb[k][:, :, :], gs_rows[k].rearrange("(t p) s -> p t s", p=P)).then_inc(s_rb[k], 16)

        GCH = 6

        def group_stats_dve(dve, k, b, up):
            n = [0]

            def link(ins):
                n[0] += 1
                ins.then_inc(s_gch[k], 1)
                dve.wait_ge(s_gch[k], b * GCH + n[0])

            mean, var = gin[k][:, :, 0], gin[k][:, :, 1]
            g = gs[k]
            dve.wait_ge(s_gin[k], b * 16 + 16)
            link(nc.vector.tensor_reduce(g[:, 0:1], mean, AX_X, ALU.add))
            link(nc.vector.tensor_scalar(g[:, 1:2], g[:, 0:1], 1.0 / GC, None, ALU.mult))
            link(nc.vector.tensor_scalar(gd[k][:, :], mean, g[:, 1:2], None, ALU.subtract))
            link(nc.vector.tensor_tensor(gq[k][:, :], gd[k][:, :], gd[k][:, :], ALU.mult))
            link(nc.vector.tensor_tensor(gd[k][:, :], gq[k][:, :], var, ALU.add))
            link(nc.vector.tensor_reduce(g[:, 2:3], gd[k][:, :], AX_X, ALU.add))
            assert n[0] == GCH
            nc.vector.tensor_scalar(g[:, 3:4], g[:, 2:3], 1.0 / GC, EPS, ALU.mult, ALU.add).then_inc(s_gvar[k], 1)
            dve.wait_ge(s_pow[k], b + 1)
            nc.vector.tensor_scalar(gout[k][:, :, 0], gd[k][:, :], 0.0, g[:, 4:5], ALU.mult, ALU.add)
            nc.vector.tensor_scalar(g[:, 5:6], g[:, 1:2], g[:, 4:5], -1.0, ALU.mult, ALU.mult).then_inc(s_gvar[k], 1)
            dve.wait_ge(s_gvar[k], b * 3 + 2)
            nc.vector.tensor_scalar(gout[k][:, :, 1], gd[k][:, :], 0.0, g[:, 5:6], ALU.mult, ALU.add).then_inc(s_gvar[k], 1)
            dve.wait_ge(s_gvar[k], b * 3 + 3)
            nc.vector.tensor_scalar(gout[k][:, :, :], gout[k][:, :, :], up, None, ALU.mult).then_inc(s_gout[k], 1)

        def group_pow(pool, k, b):
            pool.wait_ge(s_gvar[k], b * 3 + 1)
            nc.gpsimd.tensor_tensor(gs[k][:, 4:5], gs[k][:, 3:4], mhalf[:, :], ALU.pow).then_inc(s_pow[k], 1)

        @block.sync
        def _(sp):
            starts_v = []

            def chain_b(b):
                for t in range(CT):
                    sp.dma_start(x1[:, t, :], x_t[b, :, t, :]).then_inc(s_x1in, 16)
                for p in range(NP):
                    for h in (2 * p + 4, 2 * p + 5):
                        if h < NH:
                            sp.wait_ge(s_exp, b * NT + 2 * MT * (p + 1))
                            sp.dma_start(a_sb[:, h % 4, :], a_rows[h:h + 1, :].broadcast_to((P, N))).then_inc(s_a[h % 4], 16)
                    if p == NP - 1:
                        break
                    sp.wait_ge(s_dsb, b * NR + p + 1)
                    for s in (0, 1):
                        sp.dma_start(dt_sb[s * P // 2:(s + 1) * P // 2, :], d_sb[s * HD:s * HD + 1, :]).then_inc(s_dt, 16)
                    sp.wait_ge(s_rt, b * NR + p + 1)
                    sp.dma_start(r_rows.rearrange("s (a n) -> (s a) n", n=2 * N // P), dt_sb[:, :]).then_inc(s_rrow, 16)
                    sp.wait_ge(s_rrow, b * NR * 16 + 16 * (p + 1))
                    hold(sp, s_held_sp)
                    if 0 < p < NP - 2:
                        sp.wait_ge(s_olo, b * NP + p)
                    for s in (0, 1):
                        sp.dma_start(r_of[p][s * HD:(s + 1) * HD, :],
                                     r_rows[s:s + 1, :].broadcast_to((HD, N))).then_inc(s_r, 16)

            def shift_in(b, t, windows):
                sp.wait_ge(s_gst[t % 2], b * 48 + 16 * (t // 2 + 1))
                hold(sp, s_held_sp)
                if t >= 3:
                    sp.wait_ge(s_pch, b * PCH + 4 * (t - 3) + 2)
                hold(sp, s_held_sp)
                for f in windows:
                    sp.dma_start(sh_t[t % 3][f * FC:(f + 1) * FC, :],
                                 shift_rows[t * P + f * FC:t * P + (f + 1) * FC,
                                            bass.ds(start_of(t * FPT + f), N)]).then_inc(s_sh[t % 3], 16)

            def start_of(f):
                return sp.value_load(starts_i[0:1, f:f + 1], min_val=0, max_val=2 * MARGIN)

            def layer1(b, windows):
                group_stats_dma(sp, "y", b)
                for t in range(CT + 3):
                    if t < CT:
                        sp.wait_ge(s_gn, b * CT + t + 1)
                        sp.dma_start(shift_rows[t * P:(t + 1) * P, MARGIN:MARGIN + N], gn_t[t % 2]).then_inc(s_gst[t % 2], 16)
                    if 1 <= t <= CT:
                        shift_in(b, t - 1, windows)
                    if t >= 3:
                        sp.wait_ge(s_fin, b * CT + t - 1)
                        hold(sp, s_held_sp)
                        sp.dma_start(out_t[b, :, t - 3, :], x1[:, t - 3, :]).then_inc(s_out, 16)
                sp.wait_ge(s_out, b * CT * 16 + CT * 16)
                hold(sp, s_held_sp)

            def first():
                for n in range(4):
                    row = (2 * C, C)[n // 2] + n % 2 * (C // 2)
                    sp.dma_start(wkv_nat[:, n * CT // 2:(n + 1) * CT // 2, :],
                                 w_qkv[row:row + C // 2, :].rearrange("(r p) c -> p r c", p=P)).then_inc(s_wkv_in[n], 16)
                for t in range(CT):
                    sp.dma_start(x_in[:, t, :], x_t[0, :, t, :]).then_inc(s_xin[t], 16)
                group_stats_dma(sp, "x", 0)
                sp.dma_start(wp_nat, w_proj.rearrange("(r p) c -> p r c", p=P)).then_inc(s_wp_in, 16)
                sp.dma_start(bias[:, :], b_proj.rearrange("(t p) -> p t", p=P), allow_slow_non_contiguous=True).then_inc(s_small_in, 16)
                sp.dma_start(offr[0:1, :, :], offset.rearrange("(a f) s -> a f s", a=1)).then_inc(s_small_in, 16)
                for t in range(CT):
                    for f in range(FPT):
                        n = t * FPT + f
                        sp.dma_start(offc[f * FC:(f + 1) * FC, t, :],
                                     offset[n:n + 1, :].broadcast_to((FC, 2))).then_inc(s_small_in, 16)
                sp.wait_ge(s_zeros, 1)
                for t in range(CT):
                    for at_ in (0, MARGIN + N):
                        sp.dma_start(shift_rows[t * P:(t + 1) * P, at_:at_ + MARGIN], zeros).then_inc(s_pads, 16)
                sp.wait_ge(s_starts, 1)

            def body(b):
                chain_b(b)
                group_stats_dma(sp, "x", b + 1)
                layer1(b, range(FPT))

            def last(b):
                chain_b(b)
                layer1(b, range(FPT // 2))

            run(sp, first, body, last)

        @block.gpsimd
        def _(pool):
            def make_h(b):
                group_pow(pool, "x", b)
                pool.wait_ge(s_rb["x"], b * 16 + 16)
                hold(pool, s_held_pool)
                for t in range(CT):
                    nc.gpsimd.tensor_scalar(x_in[:, t, :], x_in[:, t, :], rb["x"][:, t, 0:1], rb["x"][:, t, 1:2],
                                            ALU.mult, ALU.add).then_inc(s_hf, 1)

            def phase_b(b):
                pool.wait_ge(s_kv, b * KU + KU)
                for p in range(NP):
                    for m in range(1, POOL_M):
                        i = p * 2 * MT + 2 * m + 1
                        pool.wait_ge(s_exp, b * NT + i + 1)
                        n = m
                        if n == 1:
                            if p:
                                pool.wait_ge(s_acc, (b * NP + p - 1) * NDA + add_index(1, POOL_M)[1] + 1)
                            one = ring_t[(i - 2) % RING]
                        else:
                            pool.wait_ge(s_accp, (b * NP + p) * NPA + n - 1)
                            one = acc_pool
                        nc.gpsimd.tensor_tensor(acc_pool, one, ring_t[i % RING], ALU.add).then_inc(s_accp, 1)
                    if p > 1:
                        o_first(b, p - 2)
                    if p == 0:
                        pool.wait_ge(s_x1in, b * CT * 16 + CT * 16)
                    if p < 2:
                        hold(pool, s_held_pool)
                        for t in range(p * CT // 2, (p + 1) * CT // 2):
                            nc.gpsimd.tensor_scalar(x1[:, t, :], x1[:, t, :], 1.0, bias[:, t:t + 1],
                                                    ALU.mult, ALU.add).then_inc(s_xb, 1)

            def o_first(b, p):
                pool.wait_ge(s_on, b * NP + p + 1)
                hold(pool, s_held_pool)
                nc.gpsimd.tensor_copy(o_sp[:, p, 0, :], r_of[p]).then_inc(s_ohi, 1)

            def layer1(b):
                group_pow(pool, "y", b)
                pool.wait_ge(s_rb["y"], b * 16 + 16)
                hold(pool, s_held_pool)
                for t in range(CT + 3):
                    if t < CT:
                        if t >= 2:
                            pool.wait_ge(s_gst[t % 2], b * 48 + 16 * (t // 2))
                            hold(pool, s_held_pool)
                        nc.gpsimd.tensor_scalar(gn_t[t % 2], x1[:, t, :], rb["y"][:, t, 0:1], rb["y"][:, t, 1:2],
                                                ALU.mult, ALU.add).then_inc(s_gn, 1)
                    m = t - 2
                    if 0 <= m < CT:
                        sh = sh_t[m % 3].rearrange("p (y x) -> p y x", x=W)
                        pool.wait_ge(s_sh[m % 3], b * 256 + 128 * (m // 3 + 1))
                        nc.gpsimd.tensor_tensor(sh, sh, mask[:, m:m + 1, :].broadcast_to((P, H, W)),
                                                ALU.mult).then_inc(s_msk, 1)

            def first():
                nc.gpsimd.memset(zeros, 0.0).then_inc(s_zeros, 1)
                nc.gpsimd.memset(mhalf[:, :], -0.5).then_inc(s_const, 1)
                nc.gpsimd.memset(ones[:, :], 1.0).then_inc(s_const, 1)
                nc.gpsimd.memset(ident[:, :], 0.0).then_inc(s_ident, 1)
                nc.gpsimd.iota(cols, pattern=[[1, W]], base=0, channel_multiplier=0,
                               allow_small_or_imprecise_dtypes=True).then_inc(s_const, 1)
                pool.wait_ge(s_ident, 1)
                nc.gpsimd.affine_select(out=ident[:, :], in_=ident[:, :], compare_op=ALU.not_equal, fill=1.0,
                                        base=0, pattern=[[-1, P]], channel_multiplier=1).then_inc(s_ident, 1)
                pool.wait_ge(s_const, 3)
                for n in (0, 1):
                    pool.wait_ge(s_wmax, 4 + n)
                    nc.gpsimd.partition_all_reduce(wmax_all[n], wmax[n], P, ABSMAX).then_inc(s_wall, 1)
                    if n == 0:
                        make_h(0)

            def body(b):
                phase_b(b)
                make_h(b + 1)
                layer1(b)

            def last(b):
                phase_b(b)
                layer1(b)

            run(pool, first, body, last)

        @block.scalar
        def _(act):
            def make_h(b, room_free):
                for t in range(CT):
                    act.wait_ge(s_hf, b * CT + t + 1)
                    if t == 0 and room_free is not None:
                        act.wait_ge(s_ohi, room_free)
                        act.wait_ge(s_olo, room_free)
                    nc.scalar.activation(h_sp[:, t, 0, :], x_in[:, t, :], ACT.Copy).then_inc(s_hhi, 1)

            def load_x(b, tiles):
                for t in tiles:
                    act.dma_start(x_in[:, t, :], x_t[b, :, t, :]).then_inc(s_xin[t], 16)

            def phase_a(b, layer1_b, beside=None):
                for u in range(KU):
                    c, m = divmod(u, MT)
                    lo, hi = c * HALF, min((c + 1) * HALF, C)
                    if lo < hi:
                        act.wait_ge(s_bn, b * KU + u + 1)
                        nc.scalar.activation(v_sb[:, m, lo:hi], ps[:, kv_bank[u % 4], 0:hi - lo], ACT.Copy,
                                             scale=V_DOWN).then_inc(s_vev, 1)
                    if u == AT_AT:
                        act.wait_ge(s_atp, b + 1)
                        nc.scalar.activation(at[:, :], ps_at, ACT.Copy).then_inc(s_at, 1)
                        act.wait_ge(s_at, b + 1)
                        act.dma_start(a_rows.rearrange("h (m n) -> (h m) n", n=P), at[:, :]).then_inc(s_arow, 16)
                        act.wait_ge(s_arow, b * 16 + 16)
                        for h in range(4):
                            act.dma_start(a_sb[:, h, :], a_rows[h:h + 1, :].broadcast_to((P, N))).then_inc(s_a[h], 16)
                    if layer1_b is not None and u + 1 in TAPS_AT:
                        middle_tap(layer1_b, TAPS_AT.index(u + 1))
                    if beside is not None:
                        beside(u)

            def last_o(b, p):
                act.wait_ge(s_on, b * NP + p + 1)
                nc.scalar.activation(o_sp[:, p, 0, :], r_of[p], ACT.Copy).then_inc(s_ohi, 1)

            def middle_tap(b, t):
                act.wait_ge(s_msk, b * CT + t + 1)
                if t >= 2:
                    act.wait_ge(s_fin, b * CT + t)
                nc.scalar.activation(tap_t[t % 2], sh_t[t % 3], ACT.Copy,
                                     scale=taps[:, t, 1, 1:2]).then_inc(s_tap, 1)

            def shift_in(b, t, windows):
                act.wait_ge(s_gst[t % 2], b * 48 + 16 * (t // 2 + 1))
                if t >= 3:
                    act.wait_ge(s_pch, b * PCH + 4 * (t - 3) + 2)
                for f in windows:
                    n = t * FPT + f
                    start = act.value_load(starts_i[0:1, n:n + 1], min_val=0, max_val=2 * MARGIN)
                    act.dma_start(sh_t[t % 3][f * FC:(f + 1) * FC, :],
                                  shift_rows[t * P + f * FC:t * P + (f + 1) * FC, bass.ds(start, N)]).then_inc(s_sh[t % 3], 16)

            def phase_b(b):
                for p in range(NP):
                    for m in range(MT):
                        for s in (0, 1):
                            h = 2 * p + s
                            i = (p * MT + m) * 2 + s
                            if s == 0 and m == 0 and p in (0, 2):
                                act.wait_ge(s_coef, b * 2 + p // 2 + 1)
                            if m == 0:
                                act.wait_ge(s_a[h % 4], b * 48 + 16 * (h // 4 + 1))
                            if i == RING - 3:
                                act.wait_ge(s_fin, b * CT + 1)
                            if i >= RING:
                                j = i - RING
                                pj, mj = divmod(j // 2, MT)
                                act.wait_ge(s_pv, b * (NT // 2) + j // 2 + 1)
                                by_pool, n = add_index(s, mj)
                                if by_pool:
                                    act.wait_ge(s_accp, (b * NP + pj) * NPA + n + 1)
                                else:
                                    act.wait_ge(s_acc, (b * NP + pj) * NDA + n + 1)
                            nc.scalar.activation(ring_t[i % RING], a_sb[:, h % 4, :], ACT.Exp,
                                                 scale=coef[:, h, m:m + 1]).then_inc(s_exp, 1)

            def weight_first(u):
                dst, sc, t, k, r, bank = w_unit(u)
                act.wait_ge(s_wt, u + 1)
                nc.scalar.activation(dst[0][:, k, r * 3 * P:(r + 1) * 3 * P], bank, ACT.Copy, scale=sc).then_inc(s_whi, 1)

            def beside_a(u):
                if u == 3:
                    act.wait_ge(s_scale, 2)
                if 4 <= u < 4 + WU - WKU:
                    weight_first(WKU + u - 4)
                if u == 4 + WU - WKU + 1:
                    act.wait_ge(s_sub, 1)
                    nc.scalar.activation(taps[:, :, :, :], taps[:, :, :, :], ACT.Exp, scale=-2.0).then_inc(s_tapexp, 1)

            def first():
                for n in range(4):
                    act.wait_ge(s_wkv_in[n], 16)
                    cut = slice(n * QUARTER, (n + 1) * QUARTER)
                    nc.scalar.activation(wkv_abs[:, cut], ox[:, cut], ACT.Abs).then_inc(s_wabs, 1)
                act.wait_ge(s_scale, 1)
                for u in range(WKU):
                    weight_first(u)
                make_h(0, None)
                act.wait_ge(s_wp_in, 16)
                nc.scalar.activation(wp_abs, ring_flat[:, 0:CT * C], ACT.Abs).then_inc(s_wabs, 1)
                phase_a(0, None, beside_a)
                act.wait_ge(s_pads, 2 * CT * 16)

            def body(b):
                phase_b(b)
                act.wait_ge(s_pv, b * (NT // 2) + NT // 2)
                load_x(b + 1, range(CT))
                last_o(b, NP - 2)
                last_o(b, NP - 1)
                make_h(b + 1, b * NP + NP)
                phase_a(b + 1, b)

            def last(b):
                phase_b(b)
                last_o(b, NP - 2)
                last_o(b, NP - 1)
                act.wait_ge(s_starts, 1)
                for t in range(CT + 1):
                    if t < CT:
                        shift_in(b, t, range(FPT // 2, FPT))
                    if t:
                        middle_tap(b, t - 1)

            run(act, first, body, last)

        @block.vector
        def _(dve):
            def channel_stats(k, t, halves, src):
                for j in halves:
                    nc.vector.bn_stats(bst[k][:, t, j, :], src[:, t, j * HALF:(j + 1) * HALF]).then_inc(s_bst[k], 1)

            def channel_aggregate(k, b):
                dve.wait_ge(s_bst[k], b * PU + PU)
                hold(dve, s_held_dve)
                for t in range(CT):
                    ins = nc.vector.bn_aggr(mv[k][:, t, :], bst[k][:, t, :, :].rearrange("p j s -> p (j s)"))
                ins.then_inc(s_stat[k], 1)

            def x_stats(b, tiles):
                for t in tiles:
                    dve.wait_ge(s_xin[t], b * 16 + 16)
                    channel_stats("x", t, (0, 1), x_in)

            def h_second(b, t):
                dve.wait_ge(s_hhi, b * CT + t + 1)
                nc.vector.tensor_tensor(h_sp[:, t, 1, :], x_in[:, t, :], h_sp[:, t, 0, :], ALU.subtract).then_inc(s_hlo, 1)

            def phase_a(b, layer1_b, beside=None):
                n = [0]

                def link(ins, hold=True):
                    n[0] += 1
                    ins.then_inc(s_ach, 1)
                    if hold:
                        dve.wait_ge(s_ach, b * ACH + n[0])

                for u in range(KU):
                    c, m = divmod(u, MT)
                    dve.wait_ge(s_kv, b * KU + u + 1)
                    for g in range(HPC):
                        ins = nc.vector.bn_stats(st[:, m, g, :], ps[:, kv_bank[u % 4], g * HD:(g + 1) * HD])
                    ins.then_inc(s_bn, 1)
                    if m == MT - 1:
                        dve.wait_ge(s_bn, b * KU + u + 1)
                        dst = m2[:, c * HPC:(c + 1) * HPC, :].rearrange("p g m -> p m g")
                        link(nc.vector.tensor_tensor(dm[:, :, :], st[:, :, :, 1], st[:, :, :, 4], ALU.subtract))
                        link(nc.vector.tensor_tensor(sq[:, :, :], dm[:, :, :], dm[:, :, :], ALU.mult))
                        link(nc.vector.tensor_tensor(dm[:, :, :], st[:, :, :, 2], st[:, :, :, 5], ALU.add))
                        link(nc.vector.tensor_scalar(sq[:, :, :], sq[:, :, :], HD / 4.0, None, ALU.mult))
                        link(nc.vector.tensor_tensor(dst, sq[:, :, :], dm[:, :, :], ALU.add))
                    if u == 2 * MT - 1:
                        nc.vector.tensor_scalar(av[:, :, :], m2[:, 0:NH, :], var_f[:, 0:1], None, ALU.mult).then_inc(s_av, 1)
                        k_partition_max(0)
                    if u == AT_AT:
                        k_max(b, 0)
                    if u == AT_AT + 1:
                        k_scales(b, 0)
                    if layer1_b is not None and u in TAPS_AT:
                        taps_y(layer1_b, TAPS_AT.index(u))
                    if layer1_b is not None and u - 1 in TAPS_AT:
                        taps_x(layer1_b, TAPS_AT.index(u - 1))
                    if beside is not None:
                        beside(u)
                k_partition_max(1)
                assert n[0] == ACH

            def k_partition_max(part):
                h0, h1 = KH[part]
                nc.vector.tensor_reduce(kmx[:, h0:h1], m2[:, NH + h0:NH + h1, :], AX_X, ALU.max).then_inc(s_kmx, 1)

            def k_max(b, part):
                h0, h1 = KH[part]
                dve.wait_ge(s_ktp, b * 2 + part + 1)
                nc.vector.tensor_reduce(kmx1[0:h1 - h0, :], ps_kt[0:h1 - h0, :], AX_X, ALU.max).then_inc(s_kch, 1)
                dve.wait_ge(s_kch, b * 4 + 2 * part + 1)
                nc.vector.tensor_scalar(kdiag[0:h1 - h0, 0:h1 - h0], ident[0:h1 - h0, 0:h1 - h0], kmx1[0:h1 - h0, 0:1],
                                        None, ALU.mult).then_inc(s_kdiag, 1)

            def k_scales(b, part):
                h0, h1 = KH[part]
                dve.wait_ge(s_kmp, b * 2 + part + 1)
                nc.vector.tensor_tensor(coef[:, h0:h1, :], m2[:, NH + h0:NH + h1, :],
                                        ps_km[:, 0:h1 - h0].unsqueeze(2).broadcast_to((P, h1 - h0, MT)),
                                        ALU.subtract).then_inc(s_kch, 1)
                dve.wait_ge(s_kch, b * 4 + 2 * part + 2)
                nc.vector.tensor_scalar(coef[:, h0:h1, :], coef[:, h0:h1, :], var_f8[:, 0:1], 0.0,
                                        ALU.mult, ALU.min).then_inc(s_coef, 1)

            def add_tap(b, t, n, out_, in_, k):
                nc.vector.scalar_tensor_tensor(out_, in_, k, out_, ALU.mult, ALU.add).then_inc(s_pch, 1)
                dve.wait_ge(s_pch, b * PCH + 4 * t + n)

            def taps_y(b, t):
                sh = sh_t[t % 3].rearrange("p (y x) -> p y x", x=W)
                tp = tap_t[t % 2].rearrange("p (y x) -> p y x", x=W)
                ky = taps[:, t, 1, :]
                dve.wait_ge(s_tap, b * CT + t + 1)
                add_tap(b, t, 1, tp[:, 1:H, :], sh[:, 0:H - 1, :], ky[:, 0:1])
                add_tap(b, t, 2, tp[:, 0:H - 1, :], sh[:, 1:H, :], ky[:, 2:3])

            def taps_x(b, t):
                tp = tap_t[t % 2].rearrange("p (y x) -> p y x", x=W)
                xt = x1[:, t, :].rearrange("p (y x) -> p y x", x=W)
                kx = taps[:, t, 0, :]
                add_tap(b, t, 3, xt, tp, kx[:, 1:2])
                add_tap(b, t, 4, xt[:, :, 1:W], tp[:, :, 0:W - 1], kx[:, 0:1])
                nc.vector.scalar_tensor_tensor(xt[:, :, 0:W - 1], tp[:, :, 1:W], kx[:, 2:3], xt[:, :, 0:W - 1],
                                               ALU.mult, ALU.add).then_inc(s_fin, 1)

            def d_copy(b, p):
                dve.wait_ge(s_d, b * NP + p + 1)
                if p:
                    dve.wait_ge(s_dt, b * NR * 32 + 32 * p)
                nc.vector.tensor_copy(d_sb.rearrange("p (a n) -> p a n", a=2), ps[:, 4:6, :]).then_inc(s_dsb, 1)

            def d_reciprocal(b, p):
                dve.wait_ge(s_dt, b * NR * 32 + 32 * (p + 1))
                nc.vector.reciprocal(dt_sb[:, :], dt_sb[:, :]).then_inc(s_rt, 1)

            def d_reciprocal_last(b):
                dve.wait_ge(s_d, b * NP + NP)
                for j in (0, 1):
                    nc.vector.reciprocal(r_of[NP - 1][:, j * HALF:(j + 1) * HALF], ps[:, d_bank[j], :]).then_inc(s_rlast, 1)

            def o_normalise(b, p):
                if p < NR:
                    dve.wait_ge(s_r, b * NR * 32 + 32 * (p + 1))
                else:
                    dve.wait_ge(s_rlast, b * 2 + 2)
                r2 = r_of[p].rearrange("p (a n) -> p a n", a=2)
                k = o_bank[p % 3][0]
                nc.vector.tensor_tensor(r2, ps[:, k:k + 2, :], r2, ALU.mult).then_inc(s_on, 1)

            def o_second(b, p):
                dve.wait_ge(s_ohi, b * NP + p + 1)
                nc.vector.tensor_tensor(o_sp[:, p, 1, :], r_of[p], o_sp[:, p, 0, :], ALU.subtract).then_inc(s_olo, 1)

            def phase_b(b):
                for p in range(NP):
                    done = (b * NP + p) * NDA
                    for n, (s, m) in enumerate(DVE_ADDS):
                        i = (p * MT + m) * 2 + s
                        dve.wait_ge(s_exp, b * NT + i + 1)
                        if s == 0 and m == 1:
                            one = ring_t[(i - 2) % RING]
                        elif s == 1 and m == POOL_M:
                            if p:
                                dve.wait_ge(s_d, b * NP + p)
                            dve.wait_ge(s_accp, (b * NP + p + 1) * NPA)
                            one = acc_pool
                        else:
                            dve.wait_ge(s_acc, done + add_index(s, m - 1)[1] + 1)
                            one = acc[p % 2][s]
                        nc.vector.tensor_tensor(acc[p % 2][s], one, ring_t[i % RING], ALU.add).then_inc(s_acc, 1)
                        if p == 0 and (s, m) == (0, 3):
                            k_max(b, 1)
                        if p == 0 and (s, m) == (0, 6):
                            k_scales(b, 1)
                        if p and (s, m) == (0, 3):
                            d_copy(b, p - 1)
                        if p > 1 and (s, m) == (0, 4):
                            o_normalise(b, p - 2)
                        if p and (s, m) == (0, 6):
                            d_reciprocal(b, p - 1)
                        if p > 2 and (s, m) == (0, 1):
                            o_second(b, p - 3)

            def group_end(b, with_next):
                o_second(b, NP - 3)
                d_reciprocal_last(b)
                o_normalise(b, NP - 2)
                o_normalise(b, NP - 1)
                o_second(b, NP - 2)
                o_second(b, NP - 1)
                for u in range(PU):
                    t, j = divmod(u, 2)
                    if with_next and u < CT // 2:
                        x_stats(b + 1, (2 * u, 2 * u + 1))
                    if u == 2 and with_next:
                        channel_aggregate("x", b + 1)
                    if u == 4 and with_next:
                        group_stats_dve(dve, "x", b + 1, H_UP)
                    dve.wait_ge(s_pj, b * PU + u + 1)
                    if u == 0:
                        dve.wait_ge(s_xb, b * CT + CT)
                    cut = x1[:, t, j * HALF:(j + 1) * HALF]
                    nc.vector.scalar_tensor_tensor(cut, ps[:, pj_bank[u % 4], :], proj_f[:, 0:1], cut,
                                                   ALU.mult, ALU.add).then_inc(s_x1, 1)
                    if with_next and u >= PU - CT:
                        h_second(b + 1, u - (PU - CT))
                    if u >= 3:
                        dve.wait_ge(s_x1, b * PU + u + 1)
                        for v in range(0 if u == 3 else u, u + 1):
                            channel_stats("y", v // 2, (v % 2,), x1)
                channel_aggregate("y", b)

            def first():
                n = [0]

                def link(ins):
                    n[0] += 1
                    ins.then_inc(s_set, 1)
                    dve.wait_ge(s_set, n[0])

                def weights_max(q, dst, src):
                    dve.wait_ge(s_wabs, q + 1)
                    nc.vector.tensor_reduce(dst, src, AX_X, ALU.max).then_inc(s_wmax, 1)

                def weight_second(u):
                    dst, sc, t, kt, r, bank = w_unit(u)
                    cut = slice(r * 3 * P, (r + 1) * 3 * P)
                    dve.wait_ge(s_whi, u + 1)
                    nc.vector.scalar_tensor_tensor(dst[1][:, kt, cut], bank, sc, dst[0][:, kt, cut],
                                                   ALU.mult, ALU.subtract).then_inc(s_wlo, 1)

                def weights_scale(k):
                    dve.wait_ge(s_wall, k + 1)
                    link(nc.vector.tensor_reduce(inv[:, k:k + 1], wmax_all[k], AX_X, ALU.max))
                    link(nc.vector.tensor_scalar(inv[:, k:k + 1], inv[:, k:k + 1], 1e-30, 1.0 / W_TOP, ALU.max, ALU.mult))
                    nc.vector.reciprocal(scale[:, k:k + 1], inv[:, k:k + 1]).then_inc(s_scale, 1)
                    dve.wait_ge(s_scale, k + 1)

                for q in range(4):
                    weights_max(q, wmax[0][:, q:q + 1], wkv_abs[:, q * QUARTER:(q + 1) * QUARTER])
                x_stats(0, range(1))
                weights_scale(0)
                link(nc.vector.tensor_scalar(var_f[:, :], inv[:, 0:1], inv[:, 0:1], 1.0 / ((HD - 1) * H_UP * H_UP), ALU.mult, ALU.mult))
                link(nc.vector.tensor_scalar(var_f8[:, :], var_f[:, :], float(HD) ** -0.5, None, ALU.mult))
                x_stats(0, range(1, CT))
                channel_aggregate("x", 0)
                for u in range(WKU // 2):
                    weight_second(u)
                group_stats_dve(dve, "x", 0, H_UP)
                for u in range(WKU // 2, WKU):
                    weight_second(u)
                for t in range(CT):
                    h_second(0, t)
                weights_max(4, wmax[1], wp_abs)

                def displacements():
                    dve.wait_ge(s_small_in, 16 * (2 + CT * FPT))
                    dve.wait_ge(s_const, 3)
                    link(nc.vector.tensor_scalar(offc, offc, 64.0, 4096.0, ALU.mult, ALU.min))
                    link(nc.vector.tensor_scalar(offc, offc, -4096.0, None, ALU.max))
                    link(nc.vector.tensor_scalar(offi, offc, RND, None, ALU.add))
                    link(nc.vector.tensor_scalar(offi, offi, RND, None, ALU.subtract))
                    link(nc.vector.tensor_tensor(offc, offc, offi, ALU.subtract))
                    for j in range(3):
                        link(nc.vector.tensor_scalar(taps[:, :, :, j], offc, float(j - 1), None, ALU.add))
                    nc.vector.tensor_tensor(taps[:, :, :, :], taps[:, :, :, :], taps[:, :, :, :], ALU.mult).then_inc(s_sub, 1)

                def normalise_taps():
                    dve.wait_ge(s_tapexp, 1)
                    for t in range(CT):
                        link(nc.vector.tensor_reduce(tsum[:, t, :], taps[:, t, :, :], AX_X, ALU.add))
                    link(nc.vector.reciprocal(tsum, tsum))
                    for j in range(3):
                        link(nc.vector.tensor_tensor(taps[:, :, :, j], taps[:, :, :, j], tsum, ALU.mult))

                def masks():
                    for t in range(CT):
                        link(nc.vector.tensor_scalar(mask[:, t, :], cols, offi[:, t, 0:1], 0.0, ALU.subtract, ALU.is_ge))
                        link(nc.vector.tensor_scalar(mask2[:, t, :], cols, offi[:, t, 0:1], float(W - 1), ALU.subtract, ALU.is_le))
                    link(nc.vector.tensor_tensor(mask[:, :, :], mask[:, :, :], mask2, ALU.mult))

                def window_starts():
                    link(nc.vector.tensor_scalar(offr, offr, 64.0, 4096.0, ALU.mult, ALU.min))
                    link(nc.vector.tensor_scalar(offr, offr, -4096.0, None, ALU.max))
                    link(nc.vector.tensor_scalar(offr2, offr, RND, None, ALU.add))
                    link(nc.vector.tensor_scalar(offr2, offr2, RND, None, ALU.subtract))
                    link(nc.vector.tensor_scalar(offr2, offr2, float(-W), float(W), ALU.max, ALU.min))
                    link(nc.vector.tensor_scalar(starts, offr2[:, :, 1], float(-W), float(MARGIN), ALU.mult, ALU.add))
                    link(nc.vector.tensor_tensor(starts, starts, offr2[:, :, 0], ALU.subtract))
                    nc.vector.tensor_copy(starts_i[:, :], starts).then_inc(s_starts, 1)

                def beside_a(u):
                    if u == 2:
                        weights_scale(1)
                        link(nc.vector.tensor_scalar(proj_f[:, :], inv[:, 0:1], inv[:, 1:2], 1.0 / (H_UP * V_DOWN), ALU.mult, ALU.mult))
                    if 4 <= u < 4 + WU - WKU:
                        weight_second(WKU + u - 4)
                    for at_, stage in ((16, displacements), (17, window_starts), (18, normalise_taps), (19, masks)):
                        if u == at_:
                            stage()

                phase_a(0, None, beside_a)
                dve.wait_ge(s_starts, 1)
                nc.vector.tensor_copy(kmx1[:, :], ident[0:NH, 0:1]).then_inc(s_fin, 1)

            def body(b):
                phase_b(b)
                group_end(b, True)
                group_stats_dve(dve, "y", b, 1.0)
                phase_a(b + 1, b)

            def last(b):
                phase_b(b)
                group_end(b, False)
                group_stats_dve(dve, "y", b, 1.0)
                for t in range(CT):
                    taps_y(b, t)
                    taps_x(b, t)

            run(dve, first, body, last)

        @block.tensor
        def _(pe):
            def phase_a(b, room_free, beside=None):
                for u in range(KU):
                    c, m = divmod(u, MT)
                    if u >= 4:
                        pe.wait_ge(s_bn, b * KU + u - 3)
                        if u - 4 < 2 * MT:
                            pe.wait_ge(s_vev, b * 2 * MT + u - 3)
                    else:
                        room_free(u)
                    for k in range(CT):
                        if u == 0:
                            pe.wait_ge(s_hlo, b * CT + k + 1)
                        for n, (hp, wpart) in enumerate(((0, 0), (0, 1), (1, 0))):
                            last = nc.tensor.matmul(ps[:, kv_bank[u % 4], :], h_sp[:, k, hp, m * P:(m + 1) * P],
                                                    wkv[wpart][:, k, c * HALF:(c + 1) * HALF],
                                                    start=(k == 0 and n == 0), stop=(k == CT - 1 and n == 2))
                    last.then_inc(s_kv, 1)
                    if u == AT_AT:
                        pe.wait_ge(s_av, b + 1)
                        nc.tensor.transpose(ps_at, av[:, :, :].rearrange("p h m -> p (h m)"), ident[:, :]).then_inc(s_atp, 1)
                        k_transpose(b, 0)
                    if u == AT_AT + 2:
                        k_spread(b, 0)
                    if beside is not None:
                        beside(u)

            def k_transpose(b, part):
                h0, h1 = KH[part]
                pe.wait_ge(s_kmx, b * 2 + part + 1)
                nc.tensor.transpose(ps_kt[0:h1 - h0, :], kmx[:, h0:h1], ident[:, :]).then_inc(s_ktp, 1)

            def k_spread(b, part):
                n = KH[part][1] - KH[part][0]
                pe.wait_ge(s_kdiag, b * 2 + part + 1)
                nc.tensor.matmul(ps_km[:, 0:n], ones[0:n, :], kdiag[0:n, 0:n], start=True, stop=True).then_inc(s_kmp, 1)

            def denominators(b, p):
                pe.wait_ge(s_acc, (b * NP + p + 1) * NDA)
                if p:
                    pe.wait_ge(s_dsb, b * NR + p)
                for j in (0, 1):
                    cut = slice(j * HALF, (j + 1) * HALF)
                    nc.tensor.matmul(ps[0:HD, d_bank[j], :], ones[:, 0:HD], acc[p % 2][0][:, cut], start=True, stop=True)
                    last = nc.tensor.matmul(ps[HD:P, d_bank[j], :], ones[:, 0:HD], acc[p % 2][1][:, cut], start=True, stop=True)
                last.then_inc(s_d, 1)

            def phase_b(b):
                for p in range(NP):
                    for m in range(MT):
                        i = (p * MT + m) * 2
                        pe.wait_ge(s_exp, b * NT + i + 2)
                        if m == 0 and p >= 3:
                            pe.wait_ge(s_on, b * NP + p - 2)
                        for j in (0, 1):
                            for s in (0, 1):
                                last = nc.tensor.matmul(
                                    ps[s * HD:(s + 1) * HD, o_bank[p % 3][j], :],
                                    v_sb[:, m, (2 * p + s) * HD:(2 * p + s + 1) * HD],
                                    ring_t[(i + s) % RING][:, j * HALF:(j + 1) * HALF],
                                    start=(m == 0), stop=(m == MT - 1))
                        last.then_inc(s_pv, 1)
                        if p and m == 1:
                            denominators(b, p - 1)
                        if p == 0 and m == 2:
                            k_transpose(b, 1)
                        if p == 0 and m == 4:
                            k_spread(b, 1)
                denominators(b, NP - 1)

            def project(b, u, ks):
                t, j = divmod(u, 2)
                for k in ks:
                    for n, (wpart, op) in enumerate(((0, 0), (1, 0), (0, 1))):
                        last = nc.tensor.matmul(ps[:, pj_bank[u % 4], :], wp[wpart][:, k, t * P:(t + 1) * P],
                                                o_sp[:, k, op, j * HALF:(j + 1) * HALF],
                                                start=(k == 0 and n == 0), stop=(k == CT - 1 and n == 2))
                if k == CT - 1:
                    last.then_inc(s_pj, 1)

            def phase_c(b):
                pe.wait_ge(s_olo, b * NP + NP - 2)
                for u in range(4):
                    if u >= 2:
                        pe.wait_ge(s_rlast, b * 2 + u - 1)
                    project(b, u, range(CT - 2))
                pe.wait_ge(s_olo, b * NP + NP - 1)
                for u in range(4):
                    project(b, u, [CT - 2])
                pe.wait_ge(s_olo, b * NP + NP)
                for u in range(4):
                    project(b, u, [CT - 1])
                for u in range(4, PU):
                    pe.wait_ge(s_x1, b * PU + u - 3)
                    project(b, u, range(CT))

            def first():
                pe.wait_ge(s_ident, 2)
                for u in range(WKU):
                    if u % (WKU // 4) == 0:
                        pe.wait_ge(s_wkv_in[u // (WKU // 4)], 16)
                    if u >= 4:
                        pe.wait_ge(s_wlo, u - 3)
                    transpose_weights(u)
                pe.wait_ge(s_const, 3)
                phase_a(0, lambda u: pe.wait_ge(s_wlo, WKU), beside_a)

            def transpose_weights(u):
                dst, sc, nat, k, r, bank = w_unit(u)
                for q in range(3):
                    last = nc.tensor.transpose(bank[:, q * P:(q + 1) * P], nat[:, 3 * r + q, k * P:(k + 1) * P], ident[:, :])
                last.then_inc(s_wt, 1)

            def beside_a(u):
                w = u - 3
                if 0 <= w < WU - WKU:
                    if w == 0:
                        pe.wait_ge(s_wp_in, 16)
                    if w >= 2:
                        pe.wait_ge(s_wlo, WKU + w - 1)
                    transpose_weights(WKU + w)

            def body(b):
                phase_b(b)
                phase_c(b)
                phase_a(b + 1, lambda u: pe.wait_ge(s_x1, b * PU + PU - 3 + u) if u >= 2 else None)

            def last(b):
                phase_b(b)
                phase_c(b)

            run(pe, first, body, last)


_INS = ["x", "L0_conv_W_qkv", "L0_conv_W_proj", "L0_conv_b_proj", "L1_conv_offset"]


def kernel(**inputs):
    import numpy as np
    import concourse.bacc as bacc
    from concourse.bass_utils import run_bass_kernel_spmd

    nc = bacc.Bacc("TRN2", target_bir_lowering=False, num_devices=1)
    arrays, args = {}, []
    for name in _INS:
        a = np.ascontiguousarray(inputs[name])
        arrays[f"in_{name}"] = a
        args.append(nc.dram_tensor(f"in_{name}", a.shape, mybir.dt.from_np(a.dtype), kind="ExternalInput").ap())
    y = nc.dram_tensor("out", inputs["x"].shape, F32, kind="ExternalOutput").ap()
    gn_attention_displace(nc, *args, y)
    r = run_bass_kernel_spmd(nc, [arrays], core_ids=[0])
    return r.results[0]["out"]
```
